# Optimizing a Trainium2 kernel written in Bass

```python
import numpy as np
import jax
import jax.numpy as jnp

def _softmax(x, axis=-1):
    return jax.nn.softmax(x, axis=axis)

def _gelu(x):
    return jax.nn.gelu(x, approximate=True)

def _silu(x):
    return jax.nn.silu(x)

def _sigmoid(x):
    return jax.nn.sigmoid(x)

def _layernorm(x, axis=-1, eps=1e-05):
    m = jnp.mean(x, axis=axis, keepdims=True)
    v = jnp.var(x, axis=axis, keepdims=True)
    return (x - m) / jnp.sqrt(v + eps)

def _scatter_add(tgt, idx, src, axis=0):
    return tgt.at[idx].add(src)

def _segment_sum(src, seg, n):
    return jax.ops.segment_sum(src, seg, n)
kernel_name = 'mk_dlrm_tower_d1_rec_r8_cfe735'

def setup_inputs(seed: int=0):
    np.random.seed(seed)
    _w = jnp.asarray

    def _rec_inputs():
        import jax
        import jax.numpy as jnp
        _tk = jax.random.key(seed)
        dense_ctx = jax.random.normal(jax.random.fold_in(_tk, 190), (512, 16), jnp.float32)
        ids = jnp.stack([jax.random.randint(jax.random.fold_in(_tk, 200 + f), (512,), 0, v, jnp.int32) for f, v in enumerate([1250, 125000, 12500, 12500, 12500, 125000, 125000, 12500, 1000, 1250, 1250, 125000, 1250, 1000, 1000, 12500, 125000, 1250, 12500, 125000, 1000, 125000, 1250, 1250, 125000, 1250, 12500, 125000, 125000, 1250, 125000, 12500, 125000, 125000, 1250, 125000, 1000, 1000, 12500, 12500, 12500, 12500, 1000, 1250, 1000, 1250, 1000, 1250, 1000, 12500])], axis=1)
        tbl_0 = 0.05 * jax.random.normal(jax.random.fold_in(_tk, 500 + 0), (1250, 16), jnp.float32)
        tbl_1 = 0.05 * jax.random.normal(jax.random.fold_in(_tk, 500 + 1), (125000, 16), jnp.float32)
        tbl_2 = 0.05 * jax.random.normal(jax.random.fold_in(_tk, 500 + 2), (12500, 16), jnp.float32)
        tbl_3 = 0.05 * jax.random.normal(jax.random.fold_in(_tk, 500 + 3), (12500, 16), jnp.float32)
        tbl_4 = 0.05 * jax.random.normal(jax.random.fold_in(_tk, 500 + 4), (12500, 16), jnp.float32)
        tbl_5 = 0.05 * jax.random.normal(jax.random.fold_in(_tk, 500 + 5), (125000, 16), jnp.float32)
        tbl_6 = 0.05 * jax.random.normal(jax.random.fold_in(_tk, 500 + 6), (125000, 16), jnp.float32)
        tbl_7 = 0.05 * jax.random.normal(jax.random.fold_in(_tk, 500 + 7), (12500, 16), jnp.float32)
        tbl_8 = 0.05 * jax.random.normal(jax.random.fold_in(_tk, 500 + 8), (1000, 16), jnp.float32)
        tbl_9 = 0.05 * jax.random.normal(jax.random.fold_in(_tk, 500 + 9), (1250, 16), jnp.float32)
        tbl_10 = 0.05 * jax.random.normal(jax.random.fold_in(_tk, 500 + 10), (1250, 16), jnp.float32)
        tbl_11 = 0.05 * jax.random.normal(jax.random.fold_in(_tk, 500 + 11), (125000, 16), jnp.float32)
        tbl_12 = 0.05 * jax.random.normal(jax.random.fold_in(_tk, 500 + 12), (1250, 16), jnp.float32)
        tbl_13 = 0.05 * jax.random.normal(jax.random.fold_in(_tk, 500 + 13), (1000, 16), jnp.float32)
        tbl_14 = 0.05 * jax.random.normal(jax.random.fold_in(_tk, 500 + 14), (1000, 16), jnp.float32)
        tbl_15 = 0.05 * jax.random.normal(jax.random.fold_in(_tk, 500 + 15), (12500, 16), jnp.float32)
        tbl_16 = 0.05 * jax.random.normal(jax.random.fold_in(_tk, 500 + 16), (125000, 16), jnp.float32)
        tbl_17 = 0.05 * jax.random.normal(jax.random.fold_in(_tk, 500 + 17), (1250, 16), jnp.float32)
        tbl_18 = 0.05 * jax.random.normal(jax.random.fold_in(_tk, 500 + 18), (12500, 16), jnp.float32)
        tbl_19 = 0.05 * jax.random.normal(jax.random.fold_in(_tk, 500 + 19), (125000, 16), jnp.float32)
        tbl_20 = 0.05 * jax.random.normal(jax.random.fold_in(_tk, 500 + 20), (1000, 16), jnp.float32)
        tbl_21 = 0.05 * jax.random.normal(jax.random.fold_in(_tk, 500 + 21), (125000, 16), jnp.float32)
        tbl_22 = 0.05 * jax.random.normal(jax.random.fold_in(_tk, 500 + 22), (1250, 16), jnp.float32)
        tbl_23 = 0.05 * jax.random.normal(jax.random.fold_in(_tk, 500 + 23), (1250, 16), jnp.float32)
        tbl_24 = 0.05 * jax.random.normal(jax.random.fold_in(_tk, 500 + 24), (125000, 16), jnp.float32)
        tbl_25 = 0.05 * jax.random.normal(jax.random.fold_in(_tk, 500 + 25), (1250, 16), jnp.float32)
        tbl_26 = 0.05 * jax.random.normal(jax.random.fold_in(_tk, 500 + 26), (12500, 16), jnp.float32)
        tbl_27 = 0.05 * jax.random.normal(jax.random.fold_in(_tk, 500 + 27), (125000, 16), jnp.float32)
        tbl_28 = 0.05 * jax.random.normal(jax.random.fold_in(_tk, 500 + 28), (125000, 16), jnp.float32)
        tbl_29 = 0.05 * jax.random.normal(jax.random.fold_in(_tk, 500 + 29), (1250, 16), jnp.float32)
        tbl_30 = 0.05 * jax.random.normal(jax.random.fold_in(_tk, 500 + 30), (125000, 16), jnp.float32)
        tbl_31 = 0.05 * jax.random.normal(jax.random.fold_in(_tk, 500 + 31), (12500, 16), jnp.float32)
        tbl_32 = 0.05 * jax.random.normal(jax.random.fold_in(_tk, 500 + 32), (125000, 16), jnp.float32)
        tbl_33 = 0.05 * jax.random.normal(jax.random.fold_in(_tk, 500 + 33), (125000, 16), jnp.float32)
        tbl_34 = 0.05 * jax.random.normal(jax.random.fold_in(_tk, 500 + 34), (1250, 16), jnp.float32)
        tbl_35 = 0.05 * jax.random.normal(jax.random.fold_in(_tk, 500 + 35), (125000, 16), jnp.float32)
        tbl_36 = 0.05 * jax.random.normal(jax.random.fold_in(_tk, 500 + 36), (1000, 16), jnp.float32)
        tbl_37 = 0.05 * jax.random.normal(jax.random.fold_in(_tk, 500 + 37), (1000, 16), jnp.float32)
        tbl_38 = 0.05 * jax.random.normal(jax.random.fold_in(_tk, 500 + 38), (12500, 16), jnp.float32)
        tbl_39 = 0.05 * jax.random.normal(jax.random.fold_in(_tk, 500 + 39), (12500, 16), jnp.float32)
        tbl_40 = 0.05 * jax.random.normal(jax.random.fold_in(_tk, 500 + 40), (12500, 16), jnp.float32)
        tbl_41 = 0.05 * jax.random.normal(jax.random.fold_in(_tk, 500 + 41), (12500, 16), jnp.float32)
        tbl_42 = 0.05 * jax.random.normal(jax.random.fold_in(_tk, 500 + 42), (1000, 16), jnp.float32)
        tbl_43 = 0.05 * jax.random.normal(jax.random.fold_in(_tk, 500 + 43), (1250, 16), jnp.float32)
        tbl_44 = 0.05 * jax.random.normal(jax.random.fold_in(_tk, 500 + 44), (1000, 16), jnp.float32)
        tbl_45 = 0.05 * jax.random.normal(jax.random.fold_in(_tk, 500 + 45), (1250, 16), jnp.float32)
        tbl_46 = 0.05 * jax.random.normal(jax.random.fold_in(_tk, 500 + 46), (1000, 16), jnp.float32)
        tbl_47 = 0.05 * jax.random.normal(jax.random.fold_in(_tk, 500 + 47), (1250, 16), jnp.float32)
        tbl_48 = 0.05 * jax.random.normal(jax.random.fold_in(_tk, 500 + 48), (1000, 16), jnp.float32)
        tbl_49 = 0.05 * jax.random.normal(jax.random.fold_in(_tk, 500 + 49), (12500, 16), jnp.float32)
        _rk = jax.random.fold_in(_tk, 7)
        W_top1 = 0.0283866 * jax.random.normal(jax.random.fold_in(_tk, 801), (1241, 512), jnp.float32)
        W_top2 = 0.0441942 * jax.random.normal(jax.random.fold_in(_tk, 802), (512, 256), jnp.float32)
        W_top3 = 0.0625 * jax.random.normal(jax.random.fold_in(_tk, 803), (256, 1), jnp.float32)
        b_top1 = jnp.zeros((512,), jnp.float32)
        b_top2 = jnp.zeros((256,), jnp.float32)
        return (dense_ctx, ids, tbl_0, tbl_1, tbl_2, tbl_3, tbl_4, tbl_5, tbl_6, tbl_7, tbl_8, tbl_9, tbl_10, tbl_11, tbl_12, tbl_13, tbl_14, tbl_15, tbl_16, tbl_17, tbl_18, tbl_19, tbl_20, tbl_21, tbl_22, tbl_23, tbl_24, tbl_25, tbl_26, tbl_27, tbl_28, tbl_29, tbl_30, tbl_31, tbl_32, tbl_33, tbl_34, tbl_35, tbl_36, tbl_37, tbl_38, tbl_39, tbl_40, tbl_41, tbl_42, tbl_43, tbl_44, tbl_45, tbl_46, tbl_47, tbl_48, tbl_49, W_top1, b_top1, W_top2, b_top2, W_top3)
    dense_ctx, ids, tbl_0, tbl_1, tbl_2, tbl_3, tbl_4, tbl_5, tbl_6, tbl_7, tbl_8, tbl_9, tbl_10, tbl_11, tbl_12, tbl_13, tbl_14, tbl_15, tbl_16, tbl_17, tbl_18, tbl_19, tbl_20, tbl_21, tbl_22, tbl_23, tbl_24, tbl_25, tbl_26, tbl_27, tbl_28, tbl_29, tbl_30, tbl_31, tbl_32, tbl_33, tbl_34, tbl_35, tbl_36, tbl_37, tbl_38, tbl_39, tbl_40, tbl_41, tbl_42, tbl_43, tbl_44, tbl_45, tbl_46, tbl_47, tbl_48, tbl_49, W_top1, b_top1, W_top2, b_top2, W_top3 = _rec_inputs()

    def _L0_rec_setup():
        import jax, jax.numpy as jnp
        import numpy as np
        _NUM_FIELDS = 50
        _I_IDX, _J_IDX = np.triu_indices(_NUM_FIELDS, k=1)
        key = jax.random.key(seed)
        x = jax.random.normal(key, (2048, _NUM_FIELDS, 16), dtype=jnp.float32)
        return {'x': x}
    _L0_rec_all = _L0_rec_setup()
    _L0_rec_in = {k: v for k, v in _L0_rec_all.items() if k in ()}
    del _L0_rec_all
    return {'dense_ctx': dense_ctx, 'ids': ids, 'tbl_0': tbl_0, 'tbl_1': tbl_1, 'tbl_2': tbl_2, 'tbl_3': tbl_3, 'tbl_4': tbl_4, 'tbl_5': tbl_5, 'tbl_6': tbl_6, 'tbl_7': tbl_7, 'tbl_8': tbl_8, 'tbl_9': tbl_9, 'tbl_10': tbl_10, 'tbl_11': tbl_11, 'tbl_12': tbl_12, 'tbl_13': tbl_13, 'tbl_14': tbl_14, 'tbl_15': tbl_15, 'tbl_16': tbl_16, 'tbl_17': tbl_17, 'tbl_18': tbl_18, 'tbl_19': tbl_19, 'tbl_20': tbl_20, 'tbl_21': tbl_21, 'tbl_22': tbl_22, 'tbl_23': tbl_23, 'tbl_24': tbl_24, 'tbl_25': tbl_25, 'tbl_26': tbl_26, 'tbl_27': tbl_27, 'tbl_28': tbl_28, 'tbl_29': tbl_29, 'tbl_30': tbl_30, 'tbl_31': tbl_31, 'tbl_32': tbl_32, 'tbl_33': tbl_33, 'tbl_34': tbl_34, 'tbl_35': tbl_35, 'tbl_36': tbl_36, 'tbl_37': tbl_37, 'tbl_38': tbl_38, 'tbl_39': tbl_39, 'tbl_40': tbl_40, 'tbl_41': tbl_41, 'tbl_42': tbl_42, 'tbl_43': tbl_43, 'tbl_44': tbl_44, 'tbl_45': tbl_45, 'tbl_46': tbl_46, 'tbl_47': tbl_47, 'tbl_48': tbl_48, 'tbl_49': tbl_49, 'W_top1': W_top1, 'b_top1': b_top1, 'W_top2': W_top2, 'b_top2': b_top2, 'W_top3': W_top3}

def reference(dense_ctx, ids, tbl_0, tbl_1, tbl_2, tbl_3, tbl_4, tbl_5, tbl_6, tbl_7, tbl_8, tbl_9, tbl_10, tbl_11, tbl_12, tbl_13, tbl_14, tbl_15, tbl_16, tbl_17, tbl_18, tbl_19, tbl_20, tbl_21, tbl_22, tbl_23, tbl_24, tbl_25, tbl_26, tbl_27, tbl_28, tbl_29, tbl_30, tbl_31, tbl_32, tbl_33, tbl_34, tbl_35, tbl_36, tbl_37, tbl_38, tbl_39, tbl_40, tbl_41, tbl_42, tbl_43, tbl_44, tbl_45, tbl_46, tbl_47, tbl_48, tbl_49, W_top1, b_top1, W_top2, b_top2, W_top3):
    import jax
    import jax.numpy as jnp

    def _L0_rec_ref(x):
        import jax, jax.numpy as jnp
        import numpy as np
        _NUM_FIELDS = 50
        _I_IDX, _J_IDX = np.triu_indices(_NUM_FIELDS, k=1)
        gram = jnp.einsum('bid,bjd->bij', x, x)
        return gram[:, _I_IDX, _J_IDX]
    e = jnp.stack([tbl_0[ids[:, 0]], tbl_1[ids[:, 1]], tbl_2[ids[:, 2]], tbl_3[ids[:, 3]], tbl_4[ids[:, 4]], tbl_5[ids[:, 5]], tbl_6[ids[:, 6]], tbl_7[ids[:, 7]], tbl_8[ids[:, 8]], tbl_9[ids[:, 9]], tbl_10[ids[:, 10]], tbl_11[ids[:, 11]], tbl_12[ids[:, 12]], tbl_13[ids[:, 13]], tbl_14[ids[:, 14]], tbl_15[ids[:, 15]], tbl_16[ids[:, 16]], tbl_17[ids[:, 17]], tbl_18[ids[:, 18]], tbl_19[ids[:, 19]], tbl_20[ids[:, 20]], tbl_21[ids[:, 21]], tbl_22[ids[:, 22]], tbl_23[ids[:, 23]], tbl_24[ids[:, 24]], tbl_25[ids[:, 25]], tbl_26[ids[:, 26]], tbl_27[ids[:, 27]], tbl_28[ids[:, 28]], tbl_29[ids[:, 29]], tbl_30[ids[:, 30]], tbl_31[ids[:, 31]], tbl_32[ids[:, 32]], tbl_33[ids[:, 33]], tbl_34[ids[:, 34]], tbl_35[ids[:, 35]], tbl_36[ids[:, 36]], tbl_37[ids[:, 37]], tbl_38[ids[:, 38]], tbl_39[ids[:, 39]], tbl_40[ids[:, 40]], tbl_41[ids[:, 41]], tbl_42[ids[:, 42]], tbl_43[ids[:, 43]], tbl_44[ids[:, 44]], tbl_45[ids[:, 45]], tbl_46[ids[:, 46]], tbl_47[ids[:, 47]], tbl_48[ids[:, 48]], tbl_49[ids[:, 49]]], axis=1)
    z = _L0_rec_ref(e)
    z = z.reshape(z.shape[0], -1)
    h = jnp.concatenate([z, dense_ctx], axis=1)
    h = jnp.maximum(h @ W_top1 + b_top1, 0.0)
    h = jnp.maximum(h @ W_top2 + b_top2, 0.0)
    y = h @ W_top3
    return y

_drawn_inputs = setup_inputs


def setup_inputs(seed=0):
    import zlib

    import numpy as np

    out = dict(_drawn_inputs(seed))
    spreads = {'b_top1': (0.0, 0.1), 'b_top2': (0.0, 0.1)}
    factors = {'tbl_0': 5.194,
     'tbl_1': 5.133,
     'tbl_2': 4.317,
     'tbl_3': 4.329,
     'tbl_4': 4.764,
     'tbl_5': 4.834,
     'tbl_6': 4.26,
     'tbl_7': 4.505,
     'tbl_8': 4.934,
     'tbl_9': 4.732,
     'tbl_10': 4.399,
     'tbl_11': 4.782,
     'tbl_12': 4.333,
     'tbl_13': 4.519,
     'tbl_14': 4.888,
     'tbl_15': 4.597,
     'tbl_16': 4.927,
     'tbl_17': 4.387,
     'tbl_18': 4.62,
     'tbl_19': 4.872,
     'tbl_20': 4.442,
     'tbl_21': 4.658,
     'tbl_22': 4.802,
     'tbl_23': 4.651,
     'tbl_24': 4.275,
     'tbl_25': 4.503,
     'tbl_26': 4.425,
     'tbl_27': 4.958,
     'tbl_28': 4.51,
     'tbl_29': 5.003,
     'tbl_30': 5.211,
     'tbl_31': 5.676,
     'tbl_32': 4.678,
     'tbl_33': 4.458,
     'tbl_34': 5.459,
     'tbl_35': 4.473,
     'tbl_36': 4.781,
     'tbl_37': 4.456,
     'tbl_38': 4.57,
     'tbl_39': 4.355,
     'tbl_40': 4.688,
     'tbl_41': 4.655,
     'tbl_42': 4.658,
     'tbl_43': 4.423,
     'tbl_44': 4.31,
     'tbl_45': 4.79,
     'tbl_46': 4.552,
     'tbl_47': 4.17,
     'tbl_48': 4.658,
     'tbl_49': 4.716}
    for name, (base, spread) in spreads.items():
        noise = np.random.default_rng([zlib.crc32(name.encode()), seed]).standard_normal(out[name].shape)
        drawn = base * np.exp(spread * noise) if base else spread * noise
        out[name] = jnp.asarray(drawn.astype(out[name].dtype))
    for name, factor in factors.items():
        out[name] = (out[name] * factor).astype(out[name].dtype)
    return out
```

```python
import numpy as np
import concourse.bass as bass
from concourse import mybir
from contextlib import ExitStack

P = 128
FIELDS, DIM, BATCH = 50, 16, 512
GROUPS = P // DIM
LOCALS = BATCH // GROUPS
STEP = 4
STEPS = LOCALS // STEP
SLOTS = 32
CLASSES = 2
CHUNK = 128
CHUNKS = BATCH // CHUNK
SPC = STEPS // CHUNKS
H1, H2 = 512, 256
K1 = 13

SETS = {"A": (0, 13), "B": (13, 26), "C": (26, 39), "D": (39, 50)}
LEFT = list(range(0, 50)) + list(range(0, 13))
RIGHT = list(range(13, 50)) + list(range(26, 50))
RCOL = 64
BANDS = {"A": (0, LEFT[0:39]), "D": (39, LEFT[39:63]), "B": (64, RIGHT[0:37]), "C": (101, RIGHT[37:61])}


def field_order(sizes):
    return sorted(range(len(sizes)), key=lambda f: (-sizes[f], f))


def w1_rows(order):
    pair = {}
    n = 0
    for i in range(FIELDS):
        for j in range(i + 1, FIELDS):
            pair[(i, j)] = n
            n += 1
    rows = -np.ones((P, K1), np.int64)
    for name, (lo, hi) in SETS.items():
        first, members = BANDS[name]
        for c in range(hi - lo):
            for r, m in enumerate(members):
                a, b = order[m], order[lo + c]
                key = (min(a, b), max(a, b))
                if key in pair:
                    rows[first + r, c] = pair.pop(key)
    assert not pair
    for k in range(DIM + 1):
        rows[125 + k % 3, k // 3] = n + k
    return rows


def build(nc, table, idx, offs, ident_in, rest_in, corner_in, w1_in, w2_in, b2_in, w3_in, out):
    fp32, i32 = mybir.dt.float32, mybir.dt.int32
    ALU, ACT = mybir.AluOpType, mybir.ActivationFunctionType
    with ExitStack() as ctx:
        def sb(name, shape, dt=fp32):
            return ctx.enter_context(nc.sbuf_tensor(name, shape, dt))

        def ps(name, shape):
            return ctx.enter_context(nc.psum_tensor(name, shape, fp32))

        def sem(name):
            return ctx.enter_context(nc.semaphore(name))

        NG = CLASSES * STEPS * GROUPS
        ids = sb("ids", [P, NG], i32)
        off = sb("off", [P, NG], i32)
        rows = sb("rows", [P, NG], i32)
        emb = sb("emb", [P, STEPS, CLASSES, GROUPS * DIM])
        ident = sb("ident", [P, P])
        xt = sb("xt", [P, STEPS, STEP, 128])
        NB = 4
        bd = sb("bd", [P, NB, GROUPS, STEP, FIELDS])
        z = sb("z", [P, K1, BATCH])
        w1 = sb("w1", [P, K1, H1])
        w2 = sb("w2", [P, H1 // P, H2])
        b2 = sb("b2", [P, H2])
        w3 = sb("w3", [P, H2])
        h1 = sb("h1", [P, H1])
        h1t = sb("h1t", [P, H1 // P, CHUNK])
        h2 = sb("h2", [P, H2])
        h2w = sb("h2w", [P, H2])
        y = sb("y", [P, CHUNKS])

        tr = ps("tr", [P, 2, CLASSES, P])
        gram = ps("gram", [P, 2, STEP, 256])
        h1p = ps("h1p", [P, H1])
        h1tp = ps("h1tp", [P, H1 // P, CHUNK])
        h2p = [tr]

        s_idx = sem("s_idx"); s_rows = sem("s_rows"); s_id = sem("s_id")
        s_rest = sem("s_rest"); s_w1 = sem("s_w1"); s_w2 = sem("s_w2")
        s_gat = [sem(f"s_gat{k}") for k in range(STEPS)]
        s_zero = sem("s_zero"); s_tr = sem("s_tr"); s_xt = sem("s_xt")
        s_bd = [sem(f"s_bd{k}") for k in range(NB)]
        s_gram = sem("s_gram"); s_zd = sem("s_zd"); s_zc = sem("s_zc"); s_zab = sem("s_zab")
        s_h1 = sem("s_h1"); s_relu = sem("s_relu"); s_h1t = sem("s_h1t"); s_h1c = sem("s_h1c")
        s_h2 = sem("s_h2"); s_ch = sem("s_ch"); s_y = sem("s_y"); s_out = sem("s_out")
        h2ps = ps("h2ps", [P, H2])
        block = ctx.enter_context(nc.Block())

        def gram_at(first, n, k, width, lo, cols):
            v = gram[first:first + n, k % 2, :, 0:GROUPS * width]
            return v.rearrange("p b (o j) -> p b o j", j=width)[:, :, :, lo:lo + cols]

        def z_at(first, n, k, cols):
            v = z[first:first + n, 0:cols, k * STEP * GROUPS:(k + 1) * STEP * GROUPS]
            return v.rearrange("p c (b o) -> p b o c", o=GROUPS)

        @block.gpsimd
        def _(pool):
            pool.wait_ge(s_rows, 1)
            for k in range(STEPS):
                for c in range(CLASSES):
                    for o in range(GROUPS):
                        n = (k * CLASSES + c) * GROUPS + o
                        pool.indirect_dma_start(
                            out=emb[:, k, c, o * DIM:(o + 1) * DIM], out_offset=None, in_=table[:, :],
                            in_offset=bass.IndirectOffsetOnAxis(ap=rows[:, n:n + 1], axis=0)).then_inc(s_gat[k], 16)

        def store(sp, c):
            if c < 0:
                return
            sp.wait_ge(s_y, c + 1)
            sp.dma_start(out[c * CHUNK:(c + 1) * CHUNK, :], y[:, c:c + 1]).then_inc(s_out, 16)

        @block.sync
        def _(sp):
            sp.dma_start(ids[:, :], idx).then_inc(s_idx, 16)
            sp.dma_start(off[:, :], offs).then_inc(s_idx, 16)
            sp.dma_start(ident[:, :], ident_in).then_inc(s_id, 16)
            sp.dma_start(z[125:128, :, :], rest_in[0:3]).then_inc(s_rest, 16)
            sp.dma_start(z[63:64, :, :], rest_in[3:4]).then_inc(s_rest, 16)
            sp.dma_start(z[39:63, 11:13, :], corner_in).then_inc(s_rest, 16)
            sp.dma_start(w1[:, :, :], w1_in).then_inc(s_w1, 16)
            sp.dma_start(w2[:, :, :], w2_in).then_inc(s_w2, 16)
            sp.dma_start(b2[:, :], b2_in.partition_broadcast(P)).then_inc(s_w2, 16)
            sp.dma_start(w3[:, :], w3_in.partition_broadcast(P)).then_inc(s_w2, 16)
            for k in range(STEPS):
                if k < NB:
                    sp.wait_ge(s_zero, k + 1)
                else:
                    sp.wait_ge(s_gram, k - NB + 1)
                sp.wait_ge(s_xt, k + 1)
                for o in range(GROUPS):
                    g = slice(o * DIM, (o + 1) * DIM)
                    sp.dma_start(bd[g, k % NB, o, :, :], xt[g, k, :, 13:63]).then_inc(s_bd[k % NB], 16)
                if k % SPC == 0 and k:
                    store(sp, k // SPC - 2)
            store(sp, CHUNKS - 2)
            store(sp, CHUNKS - 1)
            sp.wait_ge(s_out, 16 * CHUNKS)

        @block.tensor
        def _(pe):
            def top1(c, ks):
                if c == 0 and ks[0] == 0:
                    pe.wait_ge(s_w1, 16)
                    pe.wait_ge(s_rest, 48)
                if ks[0] == 0:
                    pe.wait_ge(s_zab, SPC * (c + 1))
                    if c:
                        pe.wait_ge(s_relu, c)
                for k in ks:
                    mm = nc.tensor.matmul(h1p[:, :], z[:, k, c * CHUNK:(c + 1) * CHUNK], w1[:, k, :],
                                          start=k == 0, stop=k == K1 - 1)
                if ks[-1] == K1 - 1:
                    mm.then_inc(s_h1, 1)

            def turn(c):
                pe.wait_ge(s_relu, c + 1)
                if c:
                    pe.wait_ge(s_h1c, c)
                for m in range(H1 // P):
                    mm = nc.tensor.transpose(h1tp[:, m, :], h1[:, m * P:(m + 1) * P], ident[:, :])
                mm.then_inc(s_h1t, 1)

            def top2(c):
                if c == 0:
                    pe.wait_ge(s_w2, 48)
                pe.wait_ge(s_h1c, c + 1)
                if c:
                    pe.wait_ge(s_y, c)
                for m in range(H1 // P):
                    mm = nc.tensor.matmul(h2ps[:, :], h1t[:, m, :], w2[:, m, :], start=m == 0, stop=m == H1 // P - 1)
                mm.then_inc(s_h2, 1)

            pe.wait_ge(s_id, 16)
            for k in range(STEPS):
                c = k // SPC - 1
                pe.wait_ge(s_gat[k], 16 * CLASSES * GROUPS)
                if k >= 2:
                    pe.wait_ge(s_xt, k - 1)
                for q in range(CLASSES):
                    mm = nc.tensor.transpose(tr[:, k % 2, q, :], emb[:, k, q, :], ident[:, :])
                mm.then_inc(s_tr, 1)
                if c >= 0:
                    if k % SPC < 3:
                        top1(c, [list(range(0, 5)), list(range(5, 9)), list(range(9, 13))][k % SPC])
                    else:
                        turn(c)
                pe.wait_ge(s_bd[k % NB], 16 * GROUPS * (k // NB + 1))
                if k >= 2:
                    pe.wait_ge(s_zab, k - 1)
                for b in range(STEP):
                    nc.tensor.matmul(gram[0:63, k % 2, b, 0:192], xt[:, k, b, 0:63], bd[:, k % NB, :, b, 26:50],
                                     start=True, stop=True)
                    mm = nc.tensor.matmul(gram[64:125, k % 2, b, 0:208], xt[:, k, b, RCOL:RCOL + 61],
                                          bd[:, k % NB, :, b, 0:26], start=True, stop=True)
                mm.then_inc(s_gram, 1)
                if c >= 0 and k % SPC == 3:
                    top2(c)
            c = CHUNKS - 1
            top1(c, list(range(K1)))
            turn(c)
            top2(c)

        @block.scalar
        def _(act):
            def relu(c):
                act.wait_ge(s_h1, c + 1)
                if c:
                    act.wait_ge(s_h1t, c)
                nc.scalar.activation(h1[:, :], h1p[:, :], ACT.Relu).then_inc(s_relu, 1)

            for k in range(STEPS):
                act.wait_ge(s_tr, k + 1)
                for q, lo, n, to in ((0, 0, 32, 0), (0, 0, 13, 50), (0, 13, 19, RCOL), (0, 26, 6, RCOL + 37),
                                     (1, 0, 18, 32), (1, 0, 18, RCOL + 19), (1, 0, 18, RCOL + 43)):
                    src = tr[:, k % 2, q, :].rearrange("p (b f) -> p b f", f=SLOTS)
                    cp = nc.scalar.copy(xt[:, k, :, to:to + n], src[:, :, lo:lo + n])
                cp.then_inc(s_xt, 1)
                if k % SPC == 2 and k > SPC:
                    relu(k // SPC - 1)
                act.wait_ge(s_gram, k + 1)
                for p0, n, j, lo, under in ((0, 39, 24, 11, s_zd), (64, 37, 26, 0, s_zc)):
                    act.wait_ge(under, k + 1)
                    cp = nc.scalar.copy(z_at(p0, n, k, 13), gram_at(p0, n, k, j, lo, 13))
                cp.then_inc(s_zab, 1)
            relu(CHUNKS - 1)

        @block.vector
        def _(dve):
            dve.wait_ge(s_idx, 32)
            nc.vector.tensor_tensor(rows[:, :], ids[:, :], off[:, :], ALU.add).then_inc(s_rows, 1)
            for k in range(NB):
                nc.vector.memset(bd[:, k], 0.0).then_inc(s_zero, 1)
            chain = [0]

            def h1_copy(c):
                dve.wait_ge(s_h1t, c + 1)
                if c:
                    dve.wait_ge(s_h2, c)
                nc.vector.tensor_copy(h1t[:, :, :], h1tp[:, :, :]).then_inc(s_h1c, 1)

            def last(c):
                dve.wait_ge(s_h2, c + 1)
                if c == 0:
                    dve.wait_ge(s_w2, 48)
                if c:
                    dve.wait_ge(s_y, c)
                nc.vector.tensor_tensor(h2[:, :], h2ps[:, :], b2[:, :], ALU.add).then_inc(s_ch, 1)
                dve.wait_ge(s_ch, c + 1)
                nc.vector.scalar_tensor_tensor(out=h2w[:, :], in0=h2[:, :], scalar=0.0, in1=w3[:, :],
                                               op0=ALU.max, op1=ALU.mult, accum_out=y[:, c:c + 1]).then_inc(s_y, 1)

            for k in range(STEPS):
                if k % SPC == 3 and k > SPC:
                    h1_copy(k // SPC - 1)
                dve.wait_ge(s_gram, k + 1)
                nc.vector.tensor_copy(z_at(32, 31, k, 11), gram_at(32, 31, k, 24, 0, 11)).then_inc(s_zd, 1)
                nc.vector.tensor_copy(z_at(96, 29, k, 13), gram_at(96, 29, k, 26, 13, 13)).then_inc(s_zc, 1)
                if k % SPC == 3 and k > SPC:
                    last(k // SPC - 1)
            h1_copy(CHUNKS - 1)
            last(CHUNKS - 1)


def kernel(**inputs):
    import concourse.bacc as bacc
    from concourse.bass_utils import run_bass_kernel_spmd as run

    nc = bacc.Bacc("TRN2", target_bir_lowering=False, num_devices=1)
    tables = [np.asarray(inputs[f"tbl_{f}"]) for f in range(FIELDS)]
    sizes = [t.shape[0] for t in tables]
    order = field_order(sizes)
    starts = np.concatenate([[0], np.cumsum([sizes[f] for f in order])])
    ids = np.asarray(inputs["ids"])
    idx = np.zeros((P, STEPS, CLASSES, GROUPS), np.int32)
    offs = np.zeros((P, STEPS, CLASSES, GROUPS), np.int32)
    grouped = ids.reshape(STEPS, STEP, GROUPS, FIELDS)
    for pos, f in enumerate(order):
        c, slot = pos // SLOTS, pos % SLOTS
        for b in range(STEP):
            idx[b * SLOTS + slot, :, c, :] = grouped[:, b, :, f]
            offs[b * SLOTS + slot, :, c, :] = starts[pos]
    dense = np.asarray(inputs["dense_ctx"])
    rest = np.zeros((4, K1, BATCH), np.float32)
    for k in range(DIM):
        rest[k % 3, k // 3] = dense[:, k]
    rest[DIM % 3, DIM // 3] = 1.0
    w = np.concatenate([np.asarray(inputs["W_top1"]), np.asarray(inputs["b_top1"])[None], np.zeros((1, H1), np.float32)])
    arrays = {
        "table": np.concatenate([tables[f] for f in order], axis=0),
        "idx": idx.reshape(P, -1),
        "offs": offs.reshape(P, -1),
        "ident": np.eye(P, dtype=np.float32),
        "rest": rest,
        "corner": np.zeros((24, 2, BATCH), np.float32),
        "w1": np.ascontiguousarray(w[w1_rows(order)]),
        "w2": np.ascontiguousarray(np.asarray(inputs["W_top2"]).reshape(H1 // P, P, H2).transpose(1, 0, 2)),
        "b2": np.asarray(inputs["b_top2"]),
        "w3": np.ascontiguousarray(np.asarray(inputs["W_top3"]).reshape(-1)),
    }
    aps = [nc.dram_tensor("in_" + n, a.shape, mybir.dt.from_np(a.dtype), kind="ExternalInput").ap() for n, a in arrays.items()]
    out = nc.dram_tensor("out", (BATCH, 1), mybir.dt.float32, kind="ExternalOutput").ap()
    build(nc, *aps, out)
    r = run(nc, [{"in_" + n: a for n, a in arrays.items()}], core_ids=[0])
    return r.results[0]["out"]
```

```python
import numpy as np
import concourse.bass as bass
from concourse import mybir
from contextlib import ExitStack

P = 128
FIELDS, DIM, BATCH = 50, 16, 512
GROUPS = P // DIM
LOCALS = BATCH // GROUPS
STEP = 4
STEPS = LOCALS // STEP
PER_STEP = STEP * GROUPS
GATHERED = P // STEP
PICKED = FIELDS - GATHERED
LOW = 8
SHORT, LONG = 1000, 1250
SHORTS = 10
LONGS = PICKED - SHORTS
TABS = PICKED + LONGS
QUAD = 32
BATCHES, PER = 3, PICKED // 3
H1, H2 = 512, 256
MS = H1 // P
K1 = 13

SETS = {"A": (0, 13), "B": (13, 26), "C": (26, 39), "D": (39, 50)}
LEFT = list(range(0, 50)) + list(range(0, 13))
RIGHT = list(range(13, 50)) + list(range(26, 50))
RCOL = 64
BANDS = {"A": (0, LEFT[0:39]), "D": (39, LEFT[39:63]),
         "B": (RCOL, RIGHT[0:37]), "C": (RCOL + 37, RIGHT[37:61])}
NL, NR = len(LEFT), len(RIGHT)
COLS = 13
WL, WR = 24, 26
SPARE = 125

CHUNKS = [range(0, 4), range(4, 8), range(8, 12), range(12, 14), range(14, 15), range(15, 16)]


def field_order(sizes):
    order = sorted(range(len(sizes)), key=lambda f: (-sizes[f], f))
    return order[:GATHERED] + sorted(order[GATHERED:], key=lambda f: (sizes[f], f))


def w1_rows(order):
    pair, n = {}, 0
    for i in range(FIELDS):
        for j in range(i + 1, FIELDS):
            pair[(i, j)] = n
            n += 1
    rows = np.full((P, K1), -1, np.int64)
    for name, (lo, hi) in SETS.items():
        first, members = BANDS[name]
        for c in range(hi - lo):
            for r, m in enumerate(members):
                a, b = order[m], order[lo + c]
                key = (min(a, b), max(a, b))
                if key in pair:
                    rows[first + r, c] = pair.pop(key)
    assert not pair
    for k in range(DIM + 1):
        rows[SPARE + k % 3, k // 3] = n + k
    return rows


C_ID, C_FOLD, C_ST64, C_ST32, C_MASK, C_Q, C_QB, C_H, C_ALL = 0, 128, 192, 256, 288, 296, 297, 298, 299


def constants():
    c = np.zeros((P, C_ALL), np.float32)
    p = np.arange(P)
    c[:, C_ID:C_ID + P] = np.eye(P)
    for odd in range(2):
        c[p, C_FOLD + QUAD * odd + DIM * odd + p % DIM] = 1
    c[p, C_ST64 + p % 64] = 1
    c[p, C_ST32 + p % 32] = 1
    c[p, C_MASK + p // DIM] = 1
    c[:, C_Q] = p
    c[:, C_QB] = P + p % QUAD
    c[:, C_H] = p // DIM
    return c


def build(nc, table, idx, offs, picked_ids, tabs_in, const_in, rest_in, zrow_in, corner_in, w1_in, w2_in, b2_in,
          w3_in, scratch, out):
    fp32, f32r = mybir.dt.float32, mybir.dt.float32r
    i32, u8 = mybir.dt.int32, mybir.dt.uint8
    ALU, ACT = mybir.AluOpType, mybir.ActivationFunctionType
    with ExitStack() as ctx:
        def sb(name, shape, dt=fp32):
            return ctx.enter_context(nc.sbuf_tensor(name, shape, dt))

        def ps(name, shape):
            return ctx.enter_context(nc.psum_tensor(name, shape, fp32))

        def sem(name):
            return ctx.enter_context(nc.semaphore(name))

        ids = sb("ids", [P, STEPS * GROUPS], i32)
        off = sb("off", [P, STEPS * GROUPS], i32)
        rows = sb("rows", [P, STEPS * GROUPS], i32)
        emb = sb("emb", [P, STEPS, GROUPS * DIM])
        const = sb("const", [P, C_ALL])
        NF = PICKED * BATCH // P
        pid = sb("pid", [P, NF], i32)
        qh32 = sb("qh32", [P, 2, NF], i32)
        qh8 = sb("qh8", [P, 2, NF], u8)
        qh = sb("qh", [P, 2, PICKED, BATCH], u8)
        qb = sb("qb", [P, 2, BATCH], u8)
        hi = sb("hi", [P, TABS, P], f32r)
        lo = sb("lo", [P, TABS, P], f32r)
        NOH, NMK = 3, 2 * PER
        onehot = sb("onehot", [P, NOH, BATCH], f32r)
        onehot_b = sb("onehot_b", [P, 2, BATCH], f32r)
        masked = sb("masked", [P, NMK, BATCH])
        xt = sb("xt", [P, STEPS, STEP, P])
        NBD = 2
        bd = sb("bd", [P, NBD, GROUPS, STEP, FIELDS])
        z = sb("z", [P, K1, BATCH])
        w1 = sb("w1", [P, K1, H1])
        w2 = sb("w2", [P, MS, H2])
        b2 = sb("b2", [P, H2])
        w3 = sb("w3", [P, H2])
        h1 = sb("h1", [P, H1])
        h1t = sb("h1t", [P, MS, P])
        h2 = sb("h2", [P, H2])
        h2w = sb("h2w", [P, H2])
        y = sb("y", [P, len(CHUNKS)])
        tabs = z[:, :, :].rearrange("p k b -> p (k b)")[:, 0:TABS * P].rearrange("p (g x) -> p g x", x=P)

        tr = ps("tr", [P, 2, 256])
        gram = ps("gram", [P, 2, STEP, 256])
        h1p = ps("h1p", [P, H1])
        h1tp = ps("h1tp", [P, MS, P])
        h2p = ps("h2p", [P, 512])
        pick = gram[:, :, :, :].rearrange("p a b n -> p (a b n)").rearrange("p (s n) -> p s n", n=BATCH)
        sums = [h1p[:, :], h1tp[:, :, :].rearrange("p m b -> p (m b)"), h2p[:, :]]

        ids_here, rows_ready = sem("ids_here"), sem("rows_ready")
        const_here, pid_here = sem("const_here"), sem("pid_here")
        tabs_here = [sem(f"tabs_here{i}") for i in range(3)]
        split, qh_ready, scratch_ready = sem("split"), sem("qh_ready"), sem("scratch_ready")
        qh_here = [sem(f"qh_here{i}") for i in range(BATCHES)]
        qb_here = sem("qb_here")
        hi_ready, lo_ready = sem("hi_ready"), sem("lo_ready")
        onehot_ready, onehot_b_ready = sem("onehot_ready"), sem("onehot_b_ready")
        picked, masked_ready = sem("picked"), sem("masked_ready")
        summed, small_ready = sem("summed"), sem("small_ready")
        rest_here, w1_here, w2_here = sem("rest_here"), sem("w1_here"), sem("w2_here")
        gathered = [sem(f"gathered{k}") for k in range(STEPS)]
        turned, xt_ready, bd_ready = sem("turned"), sem("xt_ready"), sem("bd_ready")
        gram_ready, z_d, z_c, z_ab = sem("gram_ready"), sem("z_d"), sem("z_c"), sem("z_ab")
        h1_ready, h1_copied, h1_turned, h1t_ready = sem("h1_ready"), sem("h1_copied"), sem("h1_turned"), sem("h1t_ready")
        h2_ready, h2_biased, y_ready, stored = sem("h2_ready"), sem("h2_biased"), sem("y_ready"), sem("stored")
        block = ctx.enter_context(nc.Block())

        def samples(c):
            return len(CHUNKS[c]) * PER_STEP

        def gram_at(first, n, k, width, at, cols):
            v = gram[first:first + n, k % 2, :, 0:GROUPS * width]
            return v.rearrange("p b (o j) -> p b o j", j=width)[:, :, :, at:at + cols]

        def z_at(first, n, k, cols):
            v = z[first:first + n, 0:cols, k * PER_STEP:(k + 1) * PER_STEP]
            return v.rearrange("p c (b o) -> p b o c", o=GROUPS)

        @block.gpsimd
        def _(pool):
            pool.wait_ge(rows_ready, 1)
            for k in range(STEPS):
                for o in range(GROUPS):
                    n = k * GROUPS + o
                    pool.indirect_dma_start(
                        out=emb[:, k, o * DIM:(o + 1) * DIM], out_offset=None, in_=table[:, :],
                        in_offset=bass.IndirectOffsetOnAxis(ap=rows[:, n:n + 1], axis=0)).then_inc(gathered[k], 16)

        @block.sync
        def _(sp):
            sp.dma_start(ids[:, :], idx).then_inc(ids_here, 16)
            sp.dma_start(off[:, :], offs).then_inc(ids_here, 16)
            for i, part in enumerate((slice(0, 9), slice(9, PICKED), slice(PICKED, TABS))):
                sp.dma_start(tabs[:, part, :], tabs_in[:, part, :]).then_inc(tabs_here[i], 16)
            sp.wait_ge(qh_ready, 1)
            sp.dma_start(scratch.rearrange("a (p x) -> p a x", p=P), qh8[:, :, :]).then_inc(scratch_ready, 16)
            sp.wait_ge(scratch_ready, 16)
            fields = scratch.rearrange("a (f b) -> a f b", b=BATCH)
            for i in range(BATCHES):
                f = slice(i * PER, (i + 1) * PER)
                sp.dma_start(qh[:, :, f, :], fields[:, f, :].partition_broadcast(P)).then_inc(qh_here[i], 16)
                if i == 0:
                    for j in range(P // QUAD):
                        sp.dma_start(qb[QUAD * j:QUAD * (j + 1), :, :],
                                     fields[0, SHORTS + j:PICKED:4, :].partition_broadcast(QUAD)).then_inc(qb_here, 16)
            sp.dma_start(w1[:, :, :], w1_in).then_inc(w1_here, 16)
            sp.wait_ge(lo_ready, 3)
            sp.dma_start(z[SPARE:P, :, :], rest_in).then_inc(rest_here, 16)
            sp.dma_start(z[NL:NL + 1, :, :], zrow_in).then_inc(rest_here, 16)
            sp.dma_start(z[39:NL, 11:13, :], corner_in).then_inc(rest_here, 16)
            sp.dma_start(w2[:, :, :], w2_in).then_inc(w2_here, 16)
            sp.dma_start(b2[:, :], b2_in.partition_broadcast(P)).then_inc(w2_here, 16)
            sp.dma_start(w3[:, :], w3_in.partition_broadcast(P)).then_inc(w2_here, 16)
            for c, steps in enumerate(CHUNKS):
                sp.wait_ge(y_ready, c + 1)
                at = steps[0] * PER_STEP
                sp.dma_start(out[at:at + samples(c), :], y[0:samples(c), c:c + 1]).then_inc(stored, 16)
            sp.wait_ge(stored, 16 * len(CHUNKS))

        @block.tensor
        def _(pe):
            def pick_rows(g):
                pe.wait_ge(onehot_ready, g + 1)
                pe.wait_ge(lo_ready, 1 if g < 9 else 2 if g < SHORTS else 3)
                if g >= 4:
                    pe.wait_ge(masked_ready, g - 3)
                terms = [(hi, g, onehot[:, g % NOH, :]), (lo, g, onehot[:, g % NOH, :])]
                if g >= SHORTS:
                    b = g - SHORTS
                    pe.wait_ge(onehot_b_ready, b // 4 + 1)
                    terms += [(hi, PICKED + b, onehot_b[:, b // 4, :]), (lo, PICKED + b, onehot_b[:, b // 4, :])]
                for i, (part, at, moving) in enumerate(terms):
                    mm = nc.tensor.matmul(pick[:, g % 4, :], part[:, at, :], moving,
                                          start=i == 0, stop=i == len(terms) - 1)
                mm.then_inc(picked, 1)

            def add_up(t):
                pe.wait_ge(masked_ready, PER * (t + 1))
                first = t % 2 * PER
                for odd in range(2):
                    for j in range(GROUPS // 2):
                        o = 2 * j + odd
                        mm = nc.tensor.matmul(
                            sums[t][QUAD * j:QUAD * (j + 1), 0:PER * LOCALS],
                            const[:, C_FOLD + QUAD * odd:C_FOLD + QUAD * (odd + 1)],
                            masked[:, first:first + PER, o * LOCALS:(o + 1) * LOCALS], start=odd == 0, stop=odd == 1)
                mm.then_inc(summed, 1)

            def top1(c, blocks):
                n = samples(c)
                at = CHUNKS[c][0] * PER_STEP
                if blocks[0] == 0:
                    pe.wait_ge(z_ab, CHUNKS[c][-1] + 1)
                    if c:
                        pe.wait_ge(h1_copied, c)
                    else:
                        pe.wait_ge(w1_here, 16)
                        pe.wait_ge(rest_here, 48)
                ways = P // n
                for k in blocks:
                    w = k % ways
                    mm = nc.tensor.matmul(h1p[n * w:n * (w + 1), :], z[:, k, at:at + n], w1[:, k, :],
                                          start=k < ways, stop=k + ways >= K1)
                if blocks[-1] == K1 - 1:
                    mm.then_inc(h1_ready, 1)

            def turn(c):
                n = samples(c)
                pe.wait_ge(h1_copied, c + 1)
                if c:
                    pe.wait_ge(h1t_ready, c)
                for m in range(MS):
                    part = h1[:, m * P:(m + 1) * P]
                    if n == P:
                        mm = nc.tensor.transpose(h1tp[:, m, :], part, const[:, C_ID:C_ID + P])
                    else:
                        at = {64: C_ST64, 32: C_ST32}[n]
                        mm = nc.tensor.matmul(h1tp[:, m, 0:n], part, const[:, at:at + n], start=True, stop=True)
                mm.then_inc(h1_turned, 1)

            def top2(c):
                n = samples(c)
                if c == 0:
                    pe.wait_ge(w2_here, 48)
                else:
                    pe.wait_ge(h2_biased, c)
                pe.wait_ge(h1t_ready, c + 1)
                for m in range(MS):
                    mm = nc.tensor.matmul(h2p[0:n, 0:H2], h1t[:, m, 0:n], w2[:, m, :], start=m == 0, stop=m == MS - 1)
                mm.then_inc(h2_ready, 1)

            pe.wait_ge(const_here, 16)
            for g in range(PICKED):
                pick_rows(g)
                if g % PER == 1 and g > PER:
                    add_up(g // PER - 1)
            add_up(BATCHES - 1)

            before = {4: [(top1, 0, range(0, 5))], 5: [(top1, 0, range(5, 9))], 6: [(top1, 0, range(9, K1))], 7: [(turn, 0)],
                      8: [(top1, 1, range(0, 5))], 9: [(top1, 1, range(5, 9))], 10: [(top1, 1, range(9, K1))], 11: [(turn, 1)],
                      12: [(top1, 2, range(0, 7))], 13: [(top1, 2, range(7, K1))],
                      14: [(turn, 2), (top1, 3, range(K1))], 15: [(turn, 3), (top1, 4, range(K1))]}
            after = {7: [(top2, 0)], 11: [(top2, 1)], 14: [(top2, 2)], 15: [(top2, 3)]}
            for k in range(STEPS):
                pe.wait_ge(gathered[k], 16 * GROUPS)
                if k >= 2:
                    pe.wait_ge(xt_ready, k - 1)
                nc.tensor.transpose(tr[:, k % 2, 0:P], emb[:, k, :], const[:, C_ID:C_ID + P]).then_inc(turned, 1)
                for stage, *what in before.get(k, []):
                    stage(*what)
                pe.wait_ge(bd_ready, k + 1)
                if k >= 2:
                    pe.wait_ge(z_ab, k - 1)
                for b in range(STEP):
                    nc.tensor.matmul(gram[0:NL, k % 2, b, 0:GROUPS * WL], xt[:, k, b, 0:NL],
                                     bd[:, k % NBD, :, b, FIELDS - WL:FIELDS], start=True, stop=True)
                    mm = nc.tensor.matmul(gram[RCOL:RCOL + NR, k % 2, b, 0:GROUPS * WR], xt[:, k, b, RCOL:RCOL + NR],
                                          bd[:, k % NBD, :, b, 0:WR], start=True, stop=True)
                mm.then_inc(gram_ready, 1)
                for stage, *what in after.get(k, []):
                    stage(*what)
            turn(4)
            top1(5, range(K1))
            top2(4)
            turn(5)
            top2(5)

        @block.scalar
        def _(act):
            act.dma_start(pid[:, :], picked_ids).then_inc(pid_here, 16)
            act.dma_start(const[:, :], const_in).then_inc(const_here, 16)
            for i, part in enumerate((slice(0, 9), slice(9, PICKED), slice(PICKED, TABS))):
                act.wait_ge(tabs_here[i], 16)
                nc.scalar.copy(hi[:, part, :], tabs[:, part, :]).then_inc(hi_ready, 1)
            for t in range(BATCHES):
                act.wait_ge(summed, t + 1)
                src = sums[t][:, 0:PER * LOCALS].rearrange("p (f b) -> p b f", b=LOCALS)
                for to in (GATHERED, RCOL + GATHERED - 13, RCOL + 37 + GATHERED - 26):
                    dst = xt[:, :, :, to + t * PER:to + (t + 1) * PER].rearrange("p k b f -> p (k b) f")
                    cp = nc.scalar.copy(dst, src)
                cp.then_inc(small_ready, 1)

            def copy_h1(c):
                act.wait_ge(h1_ready, c + 1)
                if c:
                    act.wait_ge(h1_turned, c)
                nc.scalar.copy(h1[:, :], h1p[:, :]).then_inc(h1_copied, 1)

            done = {6: 0, 10: 1, 13: 2, 14: 3, 15: 4}
            for k in range(STEPS):
                act.wait_ge(turned, k + 1)
                src = tr[:, k % 2, 0:P].rearrange("p (b f) -> p b f", f=GATHERED)
                for at, n, to in ((0, 32, 0), (0, 13, 50), (13, 19, RCOL), (26, 6, RCOL + 37)):
                    cp = nc.scalar.copy(xt[:, k, :, to:to + n], src[:, :, at:at + n])
                cp.then_inc(xt_ready, 1)
                if k in done:
                    copy_h1(done[k])
                act.wait_ge(gram_ready, k + 1)
                for first, n, width, at, under in ((0, 39, WL, 11, z_d), (RCOL, 37, WR, 0, z_c)):
                    act.wait_ge(under, k + 1)
                    cp = nc.scalar.copy(z_at(first, n, k, COLS), gram_at(first, n, k, width, at, COLS))
                cp.then_inc(z_ab, 1)
            copy_h1(5)

        @block.vector
        def _(dve):
            dve.wait_ge(ids_here, 32)
            nc.vector.tensor_tensor(rows[:, :], ids[:, :], off[:, :], ALU.add).then_inc(rows_ready, 1)
            dve.wait_ge(pid_here, 16)
            nc.vector.tensor_scalar(qh32[:, 0, :], pid[:, :], 3, None, ALU.logical_shift_right).then_inc(split, 1)
            nc.vector.tensor_scalar(qh32[:, 1, :], pid[:, :], LOW - 1, None, ALU.bitwise_and).then_inc(split, 1)
            dve.wait_ge(split, 2)
            nc.vector.tensor_copy(qh8[:, :, :], qh32[:, :, :]).then_inc(qh_ready, 1)
            for i, part in enumerate((slice(0, 9), slice(9, PICKED), slice(PICKED, TABS))):
                dve.wait_ge(hi_ready, i + 1)
                nc.vector.tensor_tensor(lo[:, part, :], tabs[:, part, :], hi[:, part, :].bitcast(fp32),
                                        ALU.subtract).then_inc(lo_ready, 1)
            dve.wait_ge(const_here, 16)

            def mask(g):
                dve.wait_ge(picked, g + 1)
                if g >= NMK:
                    dve.wait_ge(summed, g // PER - 1)
                nc.vector.scalar_tensor_tensor(out=masked[:, g % NMK, :], in0=qh[:, 1, g, :],
                                               scalar=const[:, C_H:C_H + 1], in1=pick[:, g % 4, :],
                                               op0=ALU.is_equal, op1=ALU.mult).then_inc(masked_ready, 1)

            for g in range(PICKED):
                if g % PER == 0:
                    dve.wait_ge(qh_here[g // PER], 16)
                if g >= NOH:
                    dve.wait_ge(picked, g - NOH + 1)
                nc.vector.tensor_scalar(onehot[:, g % NOH, :], qh[:, 0, g, :], const[:, C_Q:C_Q + 1], None,
                                        ALU.is_equal).then_inc(onehot_ready, 1)
                if g in (SHORTS - 1, SHORTS + 3):
                    dve.wait_ge(qb_here, 64)
                    b = (g + 1 - SHORTS) // 4
                    nc.vector.tensor_scalar(onehot_b[:, b, :], qb[:, b, :], const[:, C_QB:C_QB + 1], None,
                                            ALU.is_equal).then_inc(onehot_b_ready, 1)
                if g >= 2:
                    mask(g - 2)
            mask(PICKED - 2)
            mask(PICKED - 1)
            dve.wait_ge(small_ready, BATCHES)

            def relu_h1(c):
                n = samples(c)
                dve.wait_ge(h1_turned, c + 1)
                if c:
                    dve.wait_ge(h2_ready, c)
                nc.vector.tensor_scalar(h1t[:, :, 0:n], h1tp[:, :, 0:n], 0.0, None, ALU.max).then_inc(h1t_ready, 1)

            def last(c):
                n = samples(c)
                dve.wait_ge(h2_ready, c + 1)
                if c == 0:
                    dve.wait_ge(w2_here, 48)
                else:
                    dve.wait_ge(y_ready, c)
                nc.vector.tensor_tensor(h2[0:n, :], h2p[0:n, 0:H2], b2[0:n, :], ALU.add).then_inc(h2_biased, 1)
                dve.wait_ge(h2_biased, c + 1)
                nc.vector.scalar_tensor_tensor(out=h2w[0:n, :], in0=h2[0:n, :], scalar=0.0, in1=w3[0:n, :],
                                               op0=ALU.max, op1=ALU.mult, accum_out=y[0:n, c:c + 1]).then_inc(y_ready, 1)

            done = {7: 0, 11: 1, 14: 2, 15: 3}
            for k in range(STEPS):
                dve.wait_ge(xt_ready, k + 1)
                if k >= NBD:
                    dve.wait_ge(gram_ready, k - NBD + 1)
                cols = xt[:, k, :, COLS:COLS + FIELDS].unsqueeze(1).to_broadcast([P, GROUPS, STEP, FIELDS])
                own = const[:, C_MASK:C_MASK + GROUPS].unsqueeze(2).unsqueeze(3).to_broadcast([P, GROUPS, STEP, FIELDS])
                nc.vector.tensor_tensor(bd[:, k % NBD], cols, own, ALU.mult).then_inc(bd_ready, 1)
                if k in done:
                    relu_h1(done[k])
                dve.wait_ge(gram_ready, k + 1)
                nc.vector.tensor_copy(z_at(QUAD, NL - QUAD, k, 11), gram_at(QUAD, NL - QUAD, k, WL, 0, 11)).then_inc(z_d, 1)
                nc.vector.tensor_copy(z_at(96, RCOL + NR - 96, k, COLS),
                                      gram_at(96, RCOL + NR - 96, k, WR, COLS, COLS)).then_inc(z_c, 1)
                if k in done:
                    last(done[k])
            relu_h1(4)
            last(4)
            relu_h1(5)
            last(5)


def kernel(**inputs):
    import concourse.bacc as bacc
    from concourse.bass_utils import run_bass_kernel_spmd as run

    nc = bacc.Bacc("TRN2", target_bir_lowering=False, num_devices=1)
    tables = [np.asarray(inputs[f"tbl_{f}"]) for f in range(FIELDS)]
    sizes = [t.shape[0] for t in tables]
    order = field_order(sizes)
    assert [sizes[f] for f in order[GATHERED:]] == [SHORT] * SHORTS + [LONG] * LONGS
    ids = np.asarray(inputs["ids"])
    grouped = ids.reshape(STEPS, STEP, GROUPS, FIELDS)
    idx = np.ascontiguousarray(grouped[..., order[:GATHERED]].transpose(1, 3, 0, 2)).reshape(P, STEPS * GROUPS)
    starts = np.cumsum([0] + [sizes[f] for f in order[:GATHERED - 1]]).astype(np.int32)
    offs = np.ascontiguousarray(np.broadcast_to(np.tile(starts, STEP)[:, None], idx.shape))
    picked_ids = np.ascontiguousarray(
        ids.reshape(LOCALS, GROUPS, FIELDS)[..., order[GATHERED:]].transpose(2, 1, 0)).reshape(P, -1)
    tabs = np.zeros((P, TABS, LOW * DIM), np.float32)
    for g, f in enumerate(order[GATHERED:]):
        wide = np.zeros((2 * P * LOW, DIM), np.float32)
        wide[:sizes[f]] = tables[f]
        wide = wide.reshape(2, P, LOW * DIM)
        tabs[:, g] = wide[0]
        if g >= SHORTS:
            b = g - SHORTS
            tabs[QUAD * (b % 4):QUAD * (b % 4 + 1), PICKED + b] = wide[1, :QUAD]
    dense = np.asarray(inputs["dense_ctx"])
    rest = np.zeros((3, K1, BATCH), np.float32)
    for k in range(DIM):
        rest[k % 3, k // 3] = dense[:, k]
    rest[DIM % 3, DIM // 3] = 1.0
    w = np.concatenate([np.asarray(inputs["W_top1"]), np.asarray(inputs["b_top1"])[None], np.zeros((1, H1), np.float32)])
    arrays = {
        "table": np.concatenate([tables[f] for f in order[:GATHERED]], axis=0),
        "idx": idx,
        "offs": offs,
        "picked_ids": picked_ids,
        "tabs": tabs,
        "const": constants(),
        "rest": rest,
        "zrow": np.zeros((1, K1, BATCH), np.float32),
        "corner": np.zeros((NL - 39, 2, BATCH), np.float32),
        "w1": np.ascontiguousarray(w[w1_rows(order)]),
        "w2": np.ascontiguousarray(np.asarray(inputs["W_top2"]).reshape(MS, P, H2).transpose(1, 0, 2)),
        "b2": np.asarray(inputs["b_top2"]),
        "w3": np.ascontiguousarray(np.asarray(inputs["W_top3"]).reshape(-1)),
    }
    aps = [nc.dram_tensor("in_" + n, a.shape, mybir.dt.from_np(a.dtype), kind="ExternalInput").ap()
           for n, a in arrays.items()]
    scratch = nc.dram_tensor("scratch", (2, PICKED * BATCH), mybir.dt.uint8, kind="Internal").ap()
    out = nc.dram_tensor("out", (BATCH, 1), mybir.dt.float32, kind="ExternalOutput").ap()
    build(nc, *aps, scratch, out)
    r = run(nc, [{"in_" + n: a for n, a in arrays.items()}], core_ids=[0])
    return r.results[0]["out"]
```

```python
import numpy as np
import concourse.bass as bass
from concourse import mybir
from contextlib import ExitStack

P = 128
FIELDS, DIM, BATCH = 50, 16, 512
GROUPS = P // DIM
LOCALS = BATCH // GROUPS
STEP = 4
STEPS = LOCALS // STEP
PER_STEP = STEP * GROUPS
GATHERED = 27
PICKED = FIELDS - GATHERED
LOW = 8
SHORT, LONG = 1000, 1250
SHORTS = 10
LONGS = PICKED - SHORTS
TABS = PICKED + LONGS
QUAD = 32
ON_ACT = [g for g in range(PICKED) if g % 3 == 2]
ON_DVE = [g for g in range(PICKED) if g not in ON_ACT]
PER = 6
BATCHES = [range(g, min(g + PER, PICKED)) for g in range(0, PICKED, PER)]
LAST_ROWS = STEP * GATHERED
BLOCKS = -(-(STEPS - 1) * LAST_ROWS // P) + 1
BLOCK_OF = [-(-(k + 1) * LAST_ROWS // P) - 1 for k in range(STEPS - 1)] + [BLOCKS - 1]
EARLY = [*range(1, 8), 12]
H1, H2 = 512, 256
MS = H1 // P
K1 = 13

SETS = {"A": (0, 13), "B": (13, 26), "C": (26, 39), "D": (39, 50)}
LEFT = list(range(0, 50)) + list(range(0, 13))
RIGHT = list(range(13, 50)) + list(range(26, 50))
RCOL = 64
BANDS = {"A": (0, LEFT[0:39]), "D": (39, LEFT[39:63]),
         "B": (RCOL, RIGHT[0:37]), "C": (RCOL + 37, RIGHT[37:61])}
NL, NR = len(LEFT), len(RIGHT)
COLS = 13
WL, WR = 24, 26
SPARE = 125

CHUNKS = [range(0, 2), range(2, 6), range(6, 10), range(10, 14), range(14, 15), range(15, 16)]
GROUPED = [[0], [1], [2], [3], [4, 5]]
SPLIT = [2, 3]
PIECES = [slice(0, 2), slice(2, 7), slice(7, K1)]


def lower(k):
    return 6 if k in EARLY else 5


TAB_PARTS = [slice(0, 9), slice(9, PICKED), slice(PICKED, TABS)]


def field_order(sizes):
    order = sorted(range(len(sizes)), key=lambda f: (-sizes[f], f))
    return order[:GATHERED] + sorted(order[GATHERED:], key=lambda f: (sizes[f], f))


def w1_rows(order):
    pair, n = {}, 0
    for i in range(FIELDS):
        for j in range(i + 1, FIELDS):
            pair[(i, j)] = n
            n += 1
    rows = np.full((P, K1), -1, np.int64)
    for name, (lo, hi) in SETS.items():
        first, members = BANDS[name]
        for c in range(hi - lo):
            for r, m in enumerate(members):
                a, b = order[m], order[lo + c]
                key = (min(a, b), max(a, b))
                if key in pair:
                    rows[first + r, c] = pair.pop(key)
    assert not pair
    for k in range(DIM + 1):
        rows[SPARE + k % 3, k // 3] = n + k
    return rows


C_ID, C_FOLD, C_MASK, C_Q, C_QB, C_H, C_ALL = 0, 128, 192, 200, 202, 204, 205


def constants():
    c = np.zeros((P, C_ALL), np.float32)
    p = np.arange(P)
    c[:, C_ID:C_ID + P] = np.eye(P)
    for odd in range(2):
        c[p, C_FOLD + QUAD * odd + DIM * odd + p % DIM] = 1
    c[p, C_MASK + p // DIM] = 1
    c[:, C_Q], c[:, C_Q + 1] = p, -p
    c[:, C_QB], c[:, C_QB + 1] = P + p % QUAD, -(P + p % QUAD)
    c[:, C_H] = p // DIM
    return c


def build(nc, table, idx, picked_ids, tabs_in, const_in, rest_in, zrow_in, corner_in, w1_in, w2_in, b2_in,
          w3_in, scratch, out):
    fp32, f32r = mybir.dt.float32, mybir.dt.float32r
    i32, u8 = mybir.dt.int32, mybir.dt.uint8
    ALU, ACT, AX = mybir.AluOpType, mybir.ActivationFunctionType, mybir.AxisListType
    with ExitStack() as ctx:
        def sb(name, shape, dt=fp32):
            return ctx.enter_context(nc.sbuf_tensor(name, shape, dt))

        def ps(name, shape):
            return ctx.enter_context(nc.psum_tensor(name, shape, fp32))

        def sem(name):
            return ctx.enter_context(nc.semaphore(name))

        ids = sb("ids", [P, 2, BLOCKS * GROUPS], i32)
        rows = sb("rows", [P, BLOCKS * GROUPS], i32)
        emb = sb("emb", [P, BLOCKS, GROUPS * DIM])
        const = sb("const", [P, C_ALL])
        NF = PICKED * BATCH // P
        pid = sb("pid", [P, NF], i32)
        qh32 = sb("qh32", [P, 2, NF], i32)
        qh8 = sb("qh8", [P, 2, NF], u8)
        QB = -(-LONGS // 4)
        qb = sb("qb", [P, QB, BATCH], u8)
        w1 = sb("w1", [P, K1, H1])
        z = sb("z", [P, K1, BATCH])
        qh = z[:, :, :].rearrange("p k b -> p (k b)").bitcast(u8)[:, 0:2 * PICKED * BATCH]
        qh = qh.rearrange("p (a f b) -> p a f b", a=2, b=BATCH)
        flat = sb("flat", [P, (BLOCKS - 1) * P])
        xt = sb("xt", [P, STEPS, STEP, P])
        NBD = 2
        bd = sb("bd", [P, NBD, GROUPS, STEP, FIELDS])
        w2 = sb("w2", [P, MS, H2])
        b2 = sb("b2", [P, H2])
        w3 = sb("w3", [P, H2])
        h1 = sb("h1", [P, H1])
        h1s = sb("h1s", [P, MS, 64])
        h1t = sb("h1t", [P, 2, MS, P])
        h2 = sb("h2", [P, H2])
        h2w = sb("h2w", [P, H2])
        ones = sb("ones", [1, P])
        y = sb("y", [P, len(GROUPED)])
        tabs = w1[:, :, :].rearrange("p k n -> p (k n)")[:, 0:TABS * P].rearrange("p (g x) -> p g x", x=P)

        NOH, NMK = 4, 2 * PER
        with ExitStack() as picking:
            def early(name, shape, dt=fp32):
                return picking.enter_context(nc.sbuf_tensor(name, shape, dt))

            hi = early("hi", [P, TABS, P], f32r)
            lo = early("lo", [P, TABS, P], f32r)
            onehot = early("onehot", [P, NOH, BATCH], f32r)
            onehot_b = early("onehot_b", [P, 2, BATCH], f32r)
            apart = early("apart", [P, 2, BATCH])
            masked = early("masked", [P, NMK, BATCH])
        w1_hi = sb("w1_hi", [P, K1, H1], f32r)
        w1_lo = sb("w1_lo", [P, K1, H1], f32r)
        z_hi = sb("z_hi", [P, K1, P], f32r)
        z_lo = sb("z_lo", [P, K1, P], f32r)

        tr = ps("tr", [P, P])
        gram = ps("gram", [P, 2, STEP, 256])
        h1p = ps("h1p", [P, H1])
        h1tp = ps("h1tp", [P, MS, P])
        h2p = ps("h2p", [P, 512])
        pick = gram[:, :, :, :].rearrange("p a b n -> p (a b n)").rearrange("p (s n) -> p s n", n=BATCH)
        h1_of = [h1p] * (len(CHUNKS) - 1) + [gram[:, STEPS % 2, 0:2, :].rearrange("p b n -> p (b n)")]
        h2_of = [h2p] * (len(GROUPED) - 1) + [gram[:, STEPS % 2, 2, :]]
        sums = [h1p[:, :], h1tp[:, :, :].rearrange("p m b -> p (m b)"), h2p[:, :], h1p[:, :]]

        ids_here, rows_ready = sem("ids_here"), sem("rows_ready")
        const_here, pid_here = sem("const_here"), sem("pid_here")
        tabs_here = [sem(f"tabs_here{i}") for i in range(3)]
        split, qh_ready, scratch_ready = sem("split"), sem("qh_ready"), sem("scratch_ready")
        qh_here = [sem(f"qh_here{i}") for i in range(len(BATCHES))]
        qb_here = sem("qb_here")
        hi_ready, lo_ready = sem("hi_ready"), sem("lo_ready")
        onehot_act, onehot_dve, onehot_b_ready = sem("onehot_act"), sem("onehot_dve"), sem("onehot_b_ready")
        apart_ready = sem("apart_ready")
        picked, masked_ready = sem("picked"), sem("masked_ready")
        summed, small_ready = sem("summed"), sem("small_ready")
        rest_here, w2_here = sem("rest_here"), sem("w2_here")
        w1_here = [sem(f"w1_here{i}") for i in range(len(PIECES))]
        w1_hi_ready, w1_lo_ready = sem("w1_hi_ready"), sem("w1_lo_ready")
        z_hi_ready, z_lo_ready = sem("z_hi_ready"), sem("z_lo_ready")
        gathered = [sem(f"gathered{j}") for j in range(BLOCKS)]
        turned, flat_ready, xt_ready = sem("turned"), sem("flat_ready"), sem("xt_ready")
        bd_low, bd_high, h1_added = sem("bd_low"), sem("bd_high"), sem("h1_added")
        gram_ready, z_d, z_c, z_a, z_b = [sem(n) for n in ("gram_ready", "z_d", "z_c", "z_a", "z_b")]
        h1_ready, h1_copied, h1_turned, h1t_ready = sem("h1_ready"), sem("h1_copied"), sem("h1_turned"), sem("h1t_ready")
        h2_ready, h2_biased, y_ready, stored = sem("h2_ready"), sem("h2_biased"), sem("y_ready"), sem("stored")
        ones_ready = sem("ones_ready")
        block = ctx.enter_context(nc.Block())

        def samples(*chunks):
            return sum(len(CHUNKS[c]) for c in chunks) * PER_STEP

        def gram_at(first, n, k, width, at, cols):
            v = gram[first:first + n, k % 2, :, 0:GROUPS * width]
            return v.rearrange("p b (o j) -> p b o j", j=width)[:, :, :, at:at + cols]

        def z_at(first, n, k, cols):
            v = z[first:first + n, 0:cols, k * PER_STEP:(k + 1) * PER_STEP]
            return v.rearrange("p c (b o) -> p b o c", o=GROUPS)

        @block.gpsimd
        def _(pool):
            pool.wait_ge(rows_ready, 1)
            for k in range(BLOCKS):
                for o in range(GROUPS):
                    n = k * GROUPS + o
                    pool.indirect_dma_start(
                        out=emb[:, k, o * DIM:(o + 1) * DIM], out_offset=None, in_=table[:, :],
                        in_offset=bass.IndirectOffsetOnAxis(ap=rows[:, n:n + 1], axis=0)).then_inc(gathered[k], 16)

        @block.sync
        def _(sp):
            sp.dma_start(ids[:, :, :], idx).then_inc(ids_here, 16)
            sp.wait_ge(qh_ready, 1)
            sp.dma_start(scratch.rearrange("a (p x) -> p a x", p=P), qh8[:, :, :]).then_inc(scratch_ready, 16)
            sp.wait_ge(scratch_ready, 16)
            fields = scratch.rearrange("a (f b) -> a f b", b=BATCH)
            for i, f in enumerate(BATCHES):
                f = slice(f[0], f[-1] + 1)
                sp.dma_start(qh[:, :, f, :], fields[:, f, :].partition_broadcast(P)).then_inc(qh_here[i], 16)
                if i < 2:
                    sp.dma_start(tabs[:, TAB_PARTS[i + 1], :], tabs_in[:, TAB_PARTS[i + 1], :]).then_inc(tabs_here[i + 1], 16)
                if i == 0:
                    for j in range(P // QUAD):
                        own = fields[0, SHORTS + j:PICKED:4, :]
                        sp.dma_start(qb[QUAD * j:QUAD * (j + 1), 0:own.shape[0], :],
                                     own.partition_broadcast(QUAD)).then_inc(qb_here, 16)
            sp.wait_ge(lo_ready, 3)
            for i, part in enumerate(PIECES):
                sp.dma_start(w1[:, part, :], w1_in[:, part, :]).then_inc(w1_here[i], 16)
            sp.dma_start(w2[:, :, :], w2_in).then_inc(w2_here, 16)
            sp.dma_start(b2[:, :], b2_in.partition_broadcast(P)).then_inc(w2_here, 16)
            sp.dma_start(w3[:, :], w3_in.partition_broadcast(P)).then_inc(w2_here, 16)
            sp.wait_ge(masked_ready, PICKED)
            sp.dma_start(z[SPARE:P, :, :], rest_in).then_inc(rest_here, 16)
            sp.dma_start(z[NL:NL + 1, :, :], zrow_in).then_inc(rest_here, 16)
            sp.dma_start(z[39:NL, 11:13, :], corner_in).then_inc(rest_here, 16)
            for i, chunks in enumerate(GROUPED):
                sp.wait_ge(y_ready, i + 1)
                at, n = CHUNKS[chunks[0]][0] * PER_STEP, samples(*chunks)
                sp.dma_start(out[at:at + n, :], y[0:n, i:i + 1]).then_inc(stored, 16)
            sp.wait_ge(stored, 16 * len(GROUPED))

        @block.tensor
        def _(pe):
            def pick_rows(g):
                if g in ON_ACT:
                    pe.wait_ge(onehot_act, ON_ACT.index(g) + 1)
                else:
                    pe.wait_ge(onehot_dve, ON_DVE.index(g) + 1)
                pe.wait_ge(lo_ready, 1 if g < TAB_PARTS[0].stop else 2 if g < SHORTS else 3)
                if g >= 4:
                    pe.wait_ge(masked_ready, g - 3)
                terms = [(hi, g, onehot[:, g % NOH, :]), (lo, g, onehot[:, g % NOH, :])]
                if g >= SHORTS:
                    b = g - SHORTS
                    pe.wait_ge(onehot_b_ready, b // 4 + 1)
                    terms += [(hi, PICKED + b, onehot_b[:, b // 4 % 2, :]), (lo, PICKED + b, onehot_b[:, b // 4 % 2, :])]
                for i, (part, at, moving) in enumerate(terms):
                    mm = nc.tensor.matmul(pick[:, g % 4, :], part[:, at, :], moving,
                                          start=i == 0, stop=i == len(terms) - 1)
                mm.then_inc(picked, 1)

            def add_up(t):
                n = len(BATCHES[t])
                pe.wait_ge(masked_ready, BATCHES[t][-1] + 1)
                if t == 3:
                    pe.wait_ge(small_ready, 1)
                first = t % 2 * PER
                for odd in range(2):
                    for j in range(GROUPS // 2):
                        o = 2 * j + odd
                        mm = nc.tensor.matmul(
                            sums[t][QUAD * j:QUAD * (j + 1), 0:n * LOCALS],
                            const[:, C_FOLD + QUAD * odd:C_FOLD + QUAD * (odd + 1)],
                            masked[:, first:first + n, o * LOCALS:(o + 1) * LOCALS], start=odd == 0, stop=odd == 1)
                mm.then_inc(summed, 1)

            def turn_step(k):
                j = BLOCK_OF[k]
                if k and j == BLOCK_OF[k - 1]:
                    return
                pe.wait_ge(gathered[j], 16 * GROUPS)
                if j:
                    pe.wait_ge(flat_ready, j)
                nc.tensor.transpose(tr[:, :], emb[:, j, :], const[:, C_ID:C_ID + P]).then_inc(turned, 1)

            def top1(c, start=0, stop=K1):
                n = samples(c)
                at = CHUNKS[c][0] * PER_STEP
                ways = P // n
                if start == 0:
                    pe.wait_ge(z_a, CHUNKS[c][-1] + 1)
                    pe.wait_ge(z_b, CHUNKS[c][-1] + 1)
                    if 0 < c < len(CHUNKS) - 1:
                        pe.wait_ge(h1_copied, c)
                if c == 0 and start == 0:
                    pe.wait_ge(rest_here, 48)
                    for i in range(len(PIECES)):
                        pe.wait_ge(w1_here[i], 16)
                for k in range(start, stop):
                    if c not in SPLIT:
                        spare = ways > 1 and K1 % ways == 1
                        if spare and k == ways:
                            for w in range(ways):
                                cols = slice(w * H1 // ways, (w + 1) * H1 // ways)
                                nc.tensor.matmul(h1_of[c][n * w:n * (w + 1), cols], z[:, K1 - 1, at:at + n],
                                                 w1[:, K1 - 1, cols], start=False, stop=False)
                        if not (spare and k == K1 - 1):
                            w = k % ways
                            mm = nc.tensor.matmul(h1_of[c][n * w:n * (w + 1), :], z[:, k, at:at + n], w1[:, k, :],
                                                  start=k < ways, stop=k + ways >= K1 - spare)
                        continue
                    for i, part in enumerate(PIECES):
                        if k == part.start:
                            pe.wait_ge(z_lo_ready, len(PIECES) * SPLIT.index(c) + i + 1)
                            if c == SPLIT[0]:
                                pe.wait_ge(w1_lo_ready, part.stop)
                    nc.tensor.matmul(h1p[:, :], z_lo[:, k, :], w1_hi[:, k, :], start=k == 0, stop=False)
                    nc.tensor.matmul(h1p[:, :], z_hi[:, k, :], w1_lo[:, k, :], start=False, stop=False)
                    mm = nc.tensor.matmul(h1p[:, :], z_hi[:, k, :], w1_hi[:, k, :], start=False, stop=k == K1 - 1)
                if stop == K1:
                    mm.then_inc(h1_ready, 1)

            def turn(c):
                pe.wait_ge(h1_copied, c + 1)
                if c:
                    pe.wait_ge(h1t_ready, c)
                for m in range(MS):
                    mm = nc.tensor.transpose(h1tp[:, m, :], h1[:, m * P:(m + 1) * P], const[:, C_ID:C_ID + P])
                mm.then_inc(h1_turned, 1)

            def top2(i, start=0, stop=MS):
                n = samples(*GROUPED[i])
                if start == 0:
                    if i == 0:
                        pe.wait_ge(w2_here, 48)
                    elif i < len(GROUPED) - 1:
                        pe.wait_ge(h2_biased, i)
                    pe.wait_ge(h1t_ready, GROUPED[i][-1] + 1)
                for m in range(start, stop):
                    mm = nc.tensor.matmul(h2_of[i][0:n, 0:H2], h1t[:, i % 2, m, 0:n], w2[:, m, :],
                                          start=m == 0 and i < len(GROUPED) - 1, stop=m == MS - 1)
                if stop == MS:
                    mm.then_inc(h2_ready, 1)

            def start_with_bias():
                pe.wait_ge(ones_ready, 1)
                pe.wait_ge(z_a, STEPS - 1)
                pe.wait_ge(z_b, STEPS - 1)
                n = samples(*GROUPED[-1])
                nc.tensor.matmul(h2_of[-1][0:n, :], ones[:, 0:n], b2[0:1, :], start=True, stop=False)

            def multiply(k):
                pe.wait_ge(bd_low, k + 1)
                pe.wait_ge(bd_high, k + 1)
                if k >= 2:
                    pe.wait_ge(z_a, k - 1)
                    pe.wait_ge(z_b, k - 1)
                for b in range(STEP):
                    nc.tensor.matmul(gram[0:NL, k % 2, b, 0:GROUPS * WL], xt[:, k, b, 0:NL],
                                     bd[:, k % NBD, :, b, FIELDS - WL:FIELDS], start=True, stop=True)
                    mm = nc.tensor.matmul(gram[RCOL:RCOL + NR, k % 2, b, 0:GROUPS * WR], xt[:, k, b, RCOL:RCOL + NR],
                                          bd[:, k % NBD, :, b, 0:WR], start=True, stop=True)
                mm.then_inc(gram_ready, 1)

            pe.wait_ge(const_here, 16)
            for g in range(PICKED):
                pick_rows(g)
                if g % PER == 1 and g > PER:
                    add_up(g // PER - 1)
            turn_step(0)
            add_up(len(BATCHES) - 1)

            for k in range(STEPS):
                if k and k not in EARLY:
                    turn_step(k)
                if k + 1 in EARLY:
                    turn_step(k + 1)
                if k == 8:
                    top1(1, 4, 7)
                elif k == 9:
                    top1(1, 10, 12)
                elif k == 10:
                    top1(2, 0, 3)
                elif k == 11:
                    top1(2, 5, 8)
                elif k == 13:
                    top1(2, 12)
                    turn(2)
                elif k == 14:
                    top1(3, 4, 8)
                elif k == 15:
                    start_with_bias()
                    turn(3)
                    top1(4, 0, 4)
                multiply(k)
                if k == 2:
                    top1(0, 0, 4)
                elif k == 3:
                    top1(0, 4, 8)
                elif k == 4:
                    top1(0, 8)
                elif k == 5:
                    turn(0)
                elif k == 6:
                    top1(1, 0, 4)
                elif k == 7:
                    top2(0)
                elif k == 8:
                    top1(1, 7, 10)
                elif k == 9:
                    top1(1, 12)
                    turn(1)
                elif k == 10:
                    top2(1)
                    top1(2, 3, 5)
                elif k == 11:
                    top1(2, 8, 9)
                elif k == 12:
                    top1(2, 9, 12)
                elif k == 13:
                    top2(2)
                    top1(3, 0, 4)
                elif k == 14:
                    top1(3, 8)
                elif k == 15:
                    top1(4, 4)
                    top1(5, 0, 4)
                    turn(4)
                    top1(5, 4)
                    top2(3, 0, 1)
                    turn(5)
                    top2(3, 1)
                    top2(4)

        @block.scalar
        def _(act):
            act.dma_start(pid[:, :], picked_ids).then_inc(pid_here, 16)
            act.dma_start(const[:, :], const_in).then_inc(const_here, 16)
            act.dma_start(tabs[:, TAB_PARTS[0], :], tabs_in[:, TAB_PARTS[0], :]).then_inc(tabs_here[0], 16)

            def tables(i):
                act.wait_ge(tabs_here[i], 16)
                nc.scalar.copy(hi[:, TAB_PARTS[i], :], tabs[:, TAB_PARTS[i], :]).then_inc(hi_ready, 1)

            def one_hot(g):
                i = ON_ACT.index(g)
                act.wait_ge(qh_here[g // PER], 16)
                if i >= 2:
                    act.wait_ge(onehot_act, i - 1)
                nc.scalar.activation(apart[:, i % 2, :], qh[:, 0, g, :], ACT.Abs,
                                     bias=const[:, C_Q + 1:C_Q + 2]).then_inc(apart_ready, 1)
                if g >= NOH:
                    act.wait_ge(picked, g - NOH + 1)
                act.wait_ge(apart_ready, i + 1)
                nc.scalar.activation(onehot[:, g % NOH, :], apart[:, i % 2, :], ACT.Relu,
                                     bias=1.0, scale=-1.0).then_inc(onehot_act, 1)

            def place_sums(t):
                act.wait_ge(summed, t + 1)
                n, at = len(BATCHES[t]), BATCHES[t][0]
                src = sums[t][:, 0:n * LOCALS].rearrange("p (f b) -> p b f", b=LOCALS)
                for to in (GATHERED, RCOL + GATHERED - 13, RCOL + 37 + GATHERED - 26):
                    dst = xt[:, :, :, to + at:to + at + n].rearrange("p k b f -> p (k b) f")
                    cp = nc.scalar.copy(dst, src)
                cp.then_inc(small_ready, 1)

            def split_w1(*blocks):
                for k in blocks:
                    for i, part in enumerate(PIECES):
                        if k == part.start:
                            act.wait_ge(w1_here[i], 16)
                    nc.scalar.copy(w1_hi[:, k, :], w1[:, k, :]).then_inc(w1_hi_ready, 1)

            tables(0)
            act.wait_ge(const_here, 16)
            for g in range(PICKED):
                if g in ON_ACT:
                    one_hot(g)
                if g == 2:
                    tables(1)
                elif g == 5:
                    tables(2)
                if g % PER == 4 and g > PER:
                    place_sums(g // PER - 1)

            def place_left(k):
                j = BLOCK_OF[k]
                new = k == 0 or j > BLOCK_OF[k - 1]
                if new:
                    act.wait_ge(turned, j + 1)
                if j < BLOCKS - 1:
                    if new:
                        nc.scalar.copy(flat[:, j * P:(j + 1) * P], tr[:, :]).then_inc(flat_ready, 1)
                    act.wait_ge(flat_ready, j + 1)
                    src = flat[:, k * LAST_ROWS:(k + 1) * LAST_ROWS]
                else:
                    src = tr[:, 0:LAST_ROWS]
                src = src.rearrange("p (b f) -> p b f", f=GATHERED)
                nc.scalar.copy(xt[:, k, :, 0:GATHERED], src)
                nc.scalar.copy(xt[:, k, :, FIELDS:FIELDS + 13], src[:, :, 0:13]).then_inc(xt_ready, 1)
                return src

            def lay_out(k, src):
                nc.scalar.copy(xt[:, k, :, RCOL:RCOL + GATHERED - 13], src[:, :, 13:])
                nc.scalar.copy(xt[:, k, :, RCOL + 37:RCOL + 37 + GATHERED - 26], src[:, :, 26:])
                if k >= NBD:
                    act.wait_ge(gram_ready, k - NBD + 1)
                act.wait_ge(xt_ready, k + 1)
                for o in range(lower(k), GROUPS):
                    cp = nc.scalar.mul(bd[:, k % NBD, o, :, :], xt[:, k, :, COLS:COLS + FIELDS],
                                       const[:, C_MASK + o:C_MASK + o + 1])
                cp.then_inc(bd_high, 1)

            def copy_h1(c):
                act.wait_ge(h1_ready, c + 1)
                if c:
                    act.wait_ge(h1_turned, c)
                nc.scalar.copy(h1[:, :], h1_of[c][:, :]).then_inc(h1_copied, 1)


            def split_z(c):
                at = CHUNKS[c][0] * PER_STEP
                if c > SPLIT[0]:
                    act.wait_ge(h1_ready, c)
                act.wait_ge(z_b, CHUNKS[c][-1] + 1)
                act.wait_ge(z_a, CHUNKS[c][-1] + 1)
                for i in range(len(PIECES)):
                    nc.scalar.copy(z_hi[:, PIECES[i], :], z[:, PIECES[i], at:at + P]).then_inc(z_hi_ready, 1)

            first = place_left(0)
            for t in range(len(BATCHES)):
                if PER * (t + 1) + 4 >= PICKED:
                    place_sums(t)
            act.wait_ge(small_ready, len(BATCHES))
            lay_out(0, first)
            for k in range(STEPS):
                if k and k not in EARLY:
                    lay_out(k, place_left(k))
                if k + 1 in EARLY:
                    lay_out(k + 1, place_left(k + 1))
                if k == 3:
                    split_w1(0)
                elif k == 4:
                    split_w1(1)
                elif k == 5:
                    split_w1(2)
                elif k == 6:
                    split_w1(3, 4)
                elif k == 7:
                    split_w1(5, 6)
                elif k == 8:
                    split_w1(7, 8, 9)
                elif k == 9:
                    split_w1(10, 11, 12)
                act.wait_ge(gram_ready, k + 1)
                nc.scalar.copy(z_at(96, RCOL + NR - 96, k, COLS),
                               gram_at(96, RCOL + NR - 96, k, WR, COLS, COLS)).then_inc(z_c, 1)
                act.wait_ge(z_d, k + 1)
                nc.scalar.copy(z_at(0, 39, k, COLS), gram_at(0, 39, k, WL, 11, COLS)).then_inc(z_a, 1)
                if k == 4:
                    copy_h1(0)
                elif k == 9:
                    copy_h1(1)
                    split_z(2)
                elif k == 13:
                    split_z(3)
                elif k == 15:
                    copy_h1(4)
                    copy_h1(5)

        @block.vector
        def _(dve):
            nc.vector.memset(ones[:, :], 1.0).then_inc(ones_ready, 1)
            dve.wait_ge(ids_here, 16)
            nc.vector.tensor_tensor(rows[:, :], ids[:, 0, :], ids[:, 1, :], ALU.add).then_inc(rows_ready, 1)
            dve.wait_ge(pid_here, 16)
            nc.vector.tensor_scalar(qh32[:, 0, :], pid[:, :], 3, None, ALU.logical_shift_right).then_inc(split, 1)
            nc.vector.tensor_scalar(qh32[:, 1, :], pid[:, :], LOW - 1, None, ALU.bitwise_and).then_inc(split, 1)
            dve.wait_ge(split, 2)
            nc.vector.tensor_copy(qh8[:, :, :], qh32[:, :, :]).then_inc(qh_ready, 1)
            def rest_of_tables(i):
                dve.wait_ge(hi_ready, i + 1)
                nc.vector.tensor_tensor(lo[:, TAB_PARTS[i], :], tabs[:, TAB_PARTS[i], :],
                                        hi[:, TAB_PARTS[i], :].bitcast(fp32), ALU.subtract).then_inc(lo_ready, 1)

            rest_of_tables(0)
            dve.wait_ge(const_here, 16)

            def mask(g):
                dve.wait_ge(picked, g + 1)
                if g >= NMK:
                    dve.wait_ge(summed, g // PER - 1)
                nc.vector.scalar_tensor_tensor(out=masked[:, g % NMK, :], in0=qh[:, 1, g, :],
                                               scalar=const[:, C_H:C_H + 1], in1=pick[:, g % 4, :],
                                               op0=ALU.is_equal, op1=ALU.mult).then_inc(masked_ready, 1)

            def split_w1(*blocks):
                for k in blocks:
                    dve.wait_ge(w1_hi_ready, k + 1)
                    nc.vector.tensor_tensor(w1_lo[:, k, :], w1[:, k, :], w1_hi[:, k, :].bitcast(fp32),
                                            ALU.subtract).then_inc(w1_lo_ready, 1)

            for g in range(PICKED):
                if g % PER == 0:
                    dve.wait_ge(qh_here[g // PER], 16)
                if g >= SHORTS and (g - SHORTS) % 4 == 0:
                    b = (g - SHORTS) // 4
                    if b == 0:
                        dve.wait_ge(qb_here, 64)
                    if b >= 2:
                        dve.wait_ge(picked, SHORTS + 4 * (b - 1))
                    n = QUAD * min(4, LONGS - 4 * b)
                    nc.vector.tensor_scalar(onehot_b[0:n, b % 2, :], qb[0:n, b, :], const[0:n, C_QB:C_QB + 1], None,
                                            ALU.is_equal).then_inc(onehot_b_ready, 1)
                if g in ON_DVE:
                    if g >= NOH:
                        dve.wait_ge(picked, g - NOH + 1)
                    nc.vector.tensor_scalar(onehot[:, g % NOH, :], qh[:, 0, g, :], const[:, C_Q:C_Q + 1], None,
                                            ALU.is_equal).then_inc(onehot_dve, 1)
                if g >= 2:
                    mask(g - 2)
                if g == 4:
                    rest_of_tables(1)
                elif g == 7:
                    rest_of_tables(2)
            mask(PICKED - 2)
            mask(PICKED - 1)
            dve.wait_ge(small_ready, len(BATCHES))

            def spread(k):
                dve.wait_ge(xt_ready, k + 1)
                if k >= NBD:
                    dve.wait_ge(gram_ready, k - NBD + 1)
                shape = [P, lower(k), STEP, FIELDS]
                cols = xt[:, k, :, COLS:COLS + FIELDS].unsqueeze(1).to_broadcast(shape)
                own = const[:, C_MASK:C_MASK + lower(k)].unsqueeze(2).unsqueeze(3).to_broadcast(shape)
                nc.vector.tensor_tensor(bd[:, k % NBD, 0:lower(k)], cols, own, ALU.mult).then_inc(bd_low, 1)

            def copy_h1(c):
                dve.wait_ge(h1_ready, c + 1)
                dve.wait_ge(h1_turned, c)
                nc.vector.tensor_copy(h1[:, :], h1_of[c][:, :]).then_inc(h1_copied, 1)

            def relu_h1(c):
                i = [c in chunks for chunks in GROUPED].index(True)
                n, at = samples(c), samples(*[d for d in GROUPED[i] if d < c])
                dve.wait_ge(h1_turned, c + 1)
                if i >= 2 and not at:
                    dve.wait_ge(h2_ready, i - 1)
                src = h1tp[:, :, 0:n]
                if n <= P // 2:
                    parts = h1tp[:, :, :].rearrange("p m (w n) -> p m n w", n=n)
                    src = h1s[:, :, 0:n]
                    nc.vector.tensor_reduce(src, parts, AX.X, ALU.add).then_inc(h1_added, 1)
                    dve.wait_ge(h1_added, sum(samples(d) <= P // 2 for d in range(c + 1)))
                nc.vector.tensor_scalar(h1t[:, i % 2, :, at:at + n], src, 0.0, None, ALU.max).then_inc(h1t_ready, 1)

            def last(i):
                n = samples(*GROUPED[i])
                dve.wait_ge(h2_ready, i + 1)
                if i == 0:
                    dve.wait_ge(w2_here, 48)
                else:
                    dve.wait_ge(y_ready, i)
                if i < len(GROUPED) - 1:
                    nc.vector.tensor_tensor(h2[0:n, :], h2p[0:n, 0:H2], b2[0:n, :], ALU.add).then_inc(h2_biased, 1)
                    dve.wait_ge(h2_biased, i + 1)
                    biased = h2[0:n, :]
                else:
                    biased = h2_of[i][0:n, :]
                nc.vector.scalar_tensor_tensor(out=h2w[0:n, :], in0=biased, scalar=0.0, in1=w3[0:n, :],
                                               op0=ALU.max, op1=ALU.mult, accum_out=y[0:n, i:i + 1]).then_inc(y_ready, 1)

            def split_z(c):
                if c > SPLIT[0]:
                    dve.wait_ge(h1_ready, c)
                at = CHUNKS[c][0] * PER_STEP
                for i in range(len(PIECES)):
                    dve.wait_ge(z_hi_ready, len(PIECES) * SPLIT.index(c) + i + 1)
                    nc.vector.tensor_tensor(z_lo[:, PIECES[i], :], z[:, PIECES[i], at:at + P], z_hi[:, PIECES[i], :].bitcast(fp32),
                                            ALU.subtract).then_inc(z_lo_ready, 1)

            spread(0)
            for k in range(STEPS):
                if k and k not in EARLY:
                    spread(k)
                if k + 1 in EARLY:
                    spread(k + 1)
                if k == 10:
                    relu_h1(1)
                elif k == 13:
                    relu_h1(2)
                elif k == 14:
                    last(2)
                elif k == 15:
                    relu_h1(3)
                dve.wait_ge(gram_ready, k + 1)
                nc.vector.tensor_copy(z_at(QUAD, NL - QUAD, k, 11), gram_at(QUAD, NL - QUAD, k, WL, 0, 11)).then_inc(z_d, 1)
                dve.wait_ge(z_c, k + 1)
                nc.vector.tensor_copy(z_at(RCOL, 37, k, COLS), gram_at(RCOL, 37, k, WR, 0, COLS)).then_inc(z_b, 1)
                if k == 3:
                    split_w1(0)
                elif k == 4:
                    split_w1(1)
                elif k == 5:
                    relu_h1(0)
                    split_w1(2)
                elif k == 6:
                    split_w1(3, 4)
                elif k == 7:
                    last(0)
                    split_w1(5, 6)
                elif k == 8:
                    split_w1(7, 8, 9)
                elif k == 9:
                    split_z(2)
                    split_w1(10, 11, 12)
                elif k == 10:
                    last(1)
                elif k == 12:
                    copy_h1(2)
                elif k == 13:
                    split_z(3)
                elif k == 14:
                    copy_h1(3)
                elif k == 15:
                    relu_h1(4)
                    relu_h1(5)
                    last(3)
                    last(4)


def kernel(**inputs):
    import concourse.bacc as bacc
    from concourse.bass_utils import run_bass_kernel_spmd as run

    nc = bacc.Bacc("TRN2", target_bir_lowering=False, num_devices=1)
    tables = [np.asarray(inputs[f"tbl_{f}"]) for f in range(FIELDS)]
    sizes = [t.shape[0] for t in tables]
    order = field_order(sizes)
    assert [sizes[f] for f in order[GATHERED:]] == [SHORT] * SHORTS + [LONG] * LONGS
    ids = np.asarray(inputs["ids"])
    mine = ids.reshape(LOCALS, GROUPS, FIELDS)[..., order[:GATHERED]].transpose(0, 2, 1).reshape(-1, GROUPS)
    starts = np.cumsum([0] + [sizes[f] for f in order[:GATHERED - 1]]).astype(np.int32)
    begin = np.tile(starts, LOCALS)
    idx = np.zeros((2, BLOCKS * P, GROUPS), np.int32)
    for at, rows in ((0, slice(0, -LAST_ROWS)), ((BLOCKS - 1) * P, slice(-LAST_ROWS, None))):
        n = len(begin[rows])
        idx[0, at:at + n] = mine[rows]
        idx[1, at:at + n] = begin[rows, None]
    idx = np.ascontiguousarray(idx.reshape(2, BLOCKS, P, GROUPS).transpose(2, 0, 1, 3)).reshape(P, 2, -1)
    picked_ids = np.ascontiguousarray(
        ids.reshape(LOCALS, GROUPS, FIELDS)[..., order[GATHERED:]].transpose(2, 1, 0)).reshape(P, -1)
    tabs = np.zeros((P, TABS, LOW * DIM), np.float32)
    for g, f in enumerate(order[GATHERED:]):
        wide = np.zeros((2 * P * LOW, DIM), np.float32)
        wide[:sizes[f]] = tables[f]
        wide = wide.reshape(2, P, LOW * DIM)
        tabs[:, g] = wide[0]
        if g >= SHORTS:
            b = g - SHORTS
            tabs[QUAD * (b % 4):QUAD * (b % 4 + 1), PICKED + b] = wide[1, :QUAD]
    dense = np.asarray(inputs["dense_ctx"])
    rest = np.zeros((3, K1, BATCH), np.float32)
    for k in range(DIM):
        rest[k % 3, k // 3] = dense[:, k]
    rest[DIM % 3, DIM // 3] = 1.0
    w = np.concatenate([np.asarray(inputs["W_top1"]), np.asarray(inputs["b_top1"])[None], np.zeros((1, H1), np.float32)])
    arrays = {
        "table": np.concatenate([tables[f] for f in order[:GATHERED]], axis=0),
        "idx": idx,
        "picked_ids": picked_ids,
        "tabs": tabs,
        "const": constants(),
        "rest": rest,
        "zrow": np.zeros((1, K1, BATCH), np.float32),
        "corner": np.zeros((NL - 39, 2, BATCH), np.float32),
        "w1": np.ascontiguousarray(w[w1_rows(order)]),
        "w2": np.ascontiguousarray(np.asarray(inputs["W_top2"]).reshape(MS, P, H2).transpose(1, 0, 2)),
        "b2": np.asarray(inputs["b_top2"]),
        "w3": np.ascontiguousarray(np.asarray(inputs["W_top3"]).reshape(-1)),
    }
    aps = [nc.dram_tensor("in_" + n, a.shape, mybir.dt.from_np(a.dtype), kind="ExternalInput").ap()
           for n, a in arrays.items()]
    scratch = nc.dram_tensor("scratch", (2, PICKED * BATCH), mybir.dt.uint8, kind="Internal").ap()
    out = nc.dram_tensor("out", (BATCH, 1), mybir.dt.float32, kind="ExternalOutput").ap()
    build(nc, *aps, scratch, out)
    r = run(nc, [{"in_" + n: a for n, a in arrays.items()}], core_ids=[0])
    return r.results[0]["out"]
```
